# Optimizing a Trainium2 kernel written in Bass

```python
import numpy as np
import jax
import jax.numpy as jnp

def _softmax(x, axis=-1):
    return jax.nn.softmax(x, axis=axis)
def _gelu(x):
    return jax.nn.gelu(x, approximate=True)
def _silu(x):
    return jax.nn.silu(x)
def _sigmoid(x):
    return jax.nn.sigmoid(x)
def _layernorm(x, axis=-1, eps=1e-5):
    m = jnp.mean(x, axis=axis, keepdims=True)
    v = jnp.var(x, axis=axis, keepdims=True)
    return (x - m) / jnp.sqrt(v + eps)
def _scatter_add(tgt, idx, src, axis=0):
    return tgt.at[idx].add(src)
def _segment_sum(src, seg, n):
    return jax.ops.segment_sum(src, seg, n)

kernel_name = 'mk_conv_preact_d1_conv_nhwc768_04c878'

def setup_inputs(seed: int = 0):
    np.random.seed(seed)
    _w = jnp.asarray
    def _rec_inputs():
        import jax
        import jax.numpy as jnp
        _gk = jax.random.key(seed)
        x = -0.0001538 + 1 * jax.random.normal(jax.random.fold_in(_gk, 1), (8, 32, 32, 768), jnp.float32)
        return x
    x = _rec_inputs()
    def _L0_conv_setup():
        import jax, jax.numpy as jnp
        import numpy as np
        NUM_HEADS = 12
        DIM = 768
        HEAD_DIM = DIM // NUM_HEADS
        SCALE = HEAD_DIM ** (-0.5)

        def _rot_half(t):
            d = t.shape[-1] // 2
            return jnp.concatenate([-t[..., d:], t[..., :d]], axis=-1)

        def _apply_rope_cat(t, rope):
            sin, cos = jnp.split(rope, 2, axis=-1)
            return t * cos + _rot_half(t) * sin
        key = jax.random.key(seed)
        ks = jax.random.split(key, 6)
        B, H, W = (8, 32, 32)
        x = jax.random.normal(ks[0], (B, H, W, DIM), dtype=jnp.float32)
        rope = jax.random.normal(ks[1], (H * W, 2 * HEAD_DIM), dtype=jnp.float32)
        qkv_w = jax.random.normal(ks[2], (DIM, 3 * DIM), dtype=jnp.float32) * DIM ** (-0.5)
        qkv_b = jax.random.normal(ks[3], (3 * DIM,), dtype=jnp.float32) * 0.02
        proj_w = jax.random.normal(ks[4], (DIM, DIM), dtype=jnp.float32) * DIM ** (-0.5)
        proj_b = jax.random.normal(ks[5], (DIM,), dtype=jnp.float32) * 0.02
        return {'x': x, 'rope': rope, 'qkv_w': qkv_w, 'qkv_b': qkv_b, 'proj_w': proj_w, 'proj_b': proj_b}
    _L0_conv_all = _L0_conv_setup()
    _L0_conv_in = {k: v for k, v in _L0_conv_all.items() if k in ('rope', 'qkv_w', 'qkv_b', 'proj_w', 'proj_b', )}
    del _L0_conv_all

    return {
        "x": x,
        "L0_conv_rope": _L0_conv_in["rope"],
        "L0_conv_qkv_w": _L0_conv_in["qkv_w"],
        "L0_conv_qkv_b": _L0_conv_in["qkv_b"],
        "L0_conv_proj_w": _L0_conv_in["proj_w"],
        "L0_conv_proj_b": _L0_conv_in["proj_b"],
    }

def reference(x, L0_conv_rope, L0_conv_qkv_w, L0_conv_qkv_b, L0_conv_proj_w, L0_conv_proj_b):
    import jax
    import jax.numpy as jnp
    def _L0_conv_ref(x, rope, qkv_w, qkv_b, proj_w, proj_b):
        import jax, jax.numpy as jnp
        import numpy as np
        NUM_HEADS = 12
        DIM = 768
        HEAD_DIM = DIM // NUM_HEADS
        SCALE = HEAD_DIM ** (-0.5)

        def _rot_half(t):
            d = t.shape[-1] // 2
            return jnp.concatenate([-t[..., d:], t[..., :d]], axis=-1)

        def _apply_rope_cat(t, rope):
            sin, cos = jnp.split(rope, 2, axis=-1)
            return t * cos + _rot_half(t) * sin
        B, H, W, C = x.shape
        N = H * W
        nh, hd = (NUM_HEADS, HEAD_DIM)
        qkv = jnp.einsum('bnc,cd->bnd', x.reshape(B, N, C), qkv_w) + qkv_b
        qkv = qkv.reshape(B, N, 3, nh, hd).transpose(2, 0, 3, 1, 4)
        q, k, v = (qkv[0], qkv[1], qkv[2])
        q = _apply_rope_cat(q, rope)
        k = _apply_rope_cat(k, rope)
        attn = jnp.einsum('bhqd,bhkd->bhqk', q * SCALE, k)
        attn = jax.nn.softmax(attn, axis=-1)
        out = jnp.einsum('bhqk,bhkd->bhqd', attn, v)
        out = out.transpose(0, 2, 1, 3).reshape(B, H, W, C)
        return jnp.einsum('bhwc,cd->bhwd', out, proj_w) + proj_b

    def _gn(v, G=32, eps=1e-5):
        B_, H_, W_, C_ = v.shape
        g = v.reshape(B_, H_, W_, G, C_ // G)
        m = jnp.mean(g, axis=(1, 2, 4), keepdims=True)
        s = jnp.var(g, axis=(1, 2, 4), keepdims=True)
        return ((g - m) / jnp.sqrt(s + eps)).reshape(v.shape)

    def _ln_c(v, eps=1e-6):
        m = jnp.mean(v, axis=-1, keepdims=True)
        s = jnp.var(v, axis=-1, keepdims=True)
        return (v - m) / jnp.sqrt(s + eps)

    def _ln_t(v, eps=1e-5):
        m = jnp.mean(v, axis=-1, keepdims=True)
        s = jnp.var(v, axis=-1, keepdims=True)
        return (v - m) / jnp.sqrt(s + eps)

    def _to_tokens(v):
        B_, H_, W_, C_ = v.shape
        return v.reshape(B_, H_ * W_, C_)
    def _from_tokens(t, like):
        return t.reshape(like.shape)

    x = x + _L0_conv_ref(_gn(x), L0_conv_rope, L0_conv_qkv_w, L0_conv_qkv_b, L0_conv_proj_w, L0_conv_proj_b)
    return x


_drawn_inputs = setup_inputs


def setup_inputs(seed=0):
    import zlib

    import numpy as np

    out = dict(_drawn_inputs(seed))
    spreads = {}
    factors = {'L0_conv_proj_b': 2.98}
    for name, (base, spread) in spreads.items():
        noise = np.random.default_rng([zlib.crc32(name.encode()), seed]).standard_normal(out[name].shape)
        drawn = base * np.exp(spread * noise) if base else spread * noise
        out[name] = jnp.asarray(drawn.astype(out[name].dtype))
    for name, factor in factors.items():
        out[name] = (out[name] * factor).astype(out[name].dtype)
    return out
```

```python
from contextlib import ExitStack

import concourse.bass as bass
from concourse import mybir

B, N, C, H = 8, 1024, 768, 12
D = C // H
P = 128
CT = C // P
PAIRS = H // 2
GROUP = C // 32
GROUP_P = GROUP // CT
Q = 512
KT = N // P
STEPS = 2 * 2 * (KT // 2)
UNITS = 4
EPS = 1e-5
SCALE = float(D) ** -0.5
WSLOTS = PAIRS + 2
PROD = 3 * CT

MID, LAST, FINAL = "mid", "last", "final"

X_JOBS = [("tr", 1), ("q", 0), ("q", 1), ("k", 0), ("k", 1), ("v", 0), ("v", 1), ("tr", 0)]
X_FIRST = 7
V_PLAN = {8: ([("v", 0, 2)], [("v", 0, 3)]), 9: ([("v", 0, 4)], [("v", 0, 4)]), 10: ([("v", 0, 5)], []),
          11: ([("v", 1, 5)], [("v", 1, 5)]), 12: ([("v", 1, 2)], [("v", 1, 2)]),
          13: ([("v", 1, 2)], [("v", 1, 2)])}
X_PLAN = {
    MID: {0: ([], [("q", 0, 8)]), 1: ([("q", 0, 5)], [("q", 0, 5)]),
          2: ([("q", 1, 5)], [("q", 1, 5)]), 3: ([("q", 1, 4)], [("q", 1, 4)]),
          4: ([("k", 0, 5)], [("k", 0, 5)]), 5: ([("k", 0, 4)], [("k", 0, 4)]),
          6: ([("k", 1, 6)], [("k", 1, 6)]), 7: ([("k", 1, 6)], []),
          **V_PLAN},
    LAST: {4: ([("q", 0, 9)], [("q", 0, 9)]), 5: ([("q", 1, 9)], [("q", 1, 9)]),
           6: ([("k", 0, 9)], [("k", 0, 9)]), 7: ([("k", 1, 9)], [("k", 1, 9)]),
           **V_PLAN},
    FINAL: {},
}
EVAC = {
    MID: {1: ("q", 0), 3: ("q", 1), 5: ("k", 0), 7: ("k", 1), 10: ("v", 0), 13: ("v", 1)},
    LAST: {4: ("q", 0), 5: ("q", 1), 6: ("k", 0), 7: ("k", 1), 10: ("v", 0), 13: ("v", 1)},
    FINAL: {},
}


def mx(head, half, i, nxt=False):
    return [("max", head, half, i, nxt)]


Y_PLAN = {
    0: ([], mx(0, 1, 2), mx(0, 1, 3), []),
    1: (mx(0, 1, 4), mx(0, 1, 5), mx(0, 1, 6), []),
    2: (mx(0, 1, 7), [("row", 0, 1, False)], [], [("sum", -1)]),
    3: (mx(1, 0, 0), mx(1, 0, 1), mx(1, 0, 2), []),
    4: (mx(1, 0, 3), mx(1, 0, 4), mx(1, 0, 5), []),
    5: (mx(1, 0, 6), mx(1, 0, 7), [("row", 1, 0, False)], []),
    6: ([("sum", 0)], [], mx(1, 1, 0), mx(1, 1, 1)),
    7: (mx(1, 1, 2), mx(1, 1, 3), [], []),
    8: (mx(1, 1, 4), mx(1, 1, 5), mx(1, 1, 6), []),
    9: (mx(1, 1, 7), [("row", 1, 1, False)], [], []),
    10: ([], [("sum", 1)], [], []),
    11: ([], [], mx(0, 0, 0, True), []),
    12: (mx(0, 0, 1, True), mx(0, 0, 2, True), mx(0, 0, 3, True), [("sum", 2)]),
    13: (mx(0, 0, 4, True), mx(0, 0, 5, True), mx(0, 0, 6, True), []),
    14: (mx(0, 0, 7, True), [("row", 0, 0, True)], [], []),
    15: (mx(0, 1, 0, True), [], mx(0, 1, 1, True), []),
}
Y_FIRST = 11


def y_plan(kind):
    keep = lambda jobs: [j for j in jobs if kind != FINAL or j[-1] is not True]
    return [tuple(keep(jobs) for jobs in Y_PLAN.get(s, ([], [], [], []))) for s in range(STEPS)]


def y_index(kind):
    order = [j for places in y_plan(kind) for jobs in places for j in jobs]
    return {j: n for n, j in enumerate(order)}


Y_JOBS = len(y_index(MID))
Y_LAST = len(y_index(FINAL))
ROW_0 = y_index(MID)[("row", 0, 0, True)]
POOL_SETUP, DVE_SETUP = 6, 8


def ahead(eng, *values):
    for value in values:
        if not isinstance(value, int):
            eng.to_reg(value)
    return values


def each_iteration(eng, body):
    with eng.Fori(0, B - 1) as b:
        with eng.Fori(0, PAIRS - 1) as p:
            body(b * PAIRS + p, b, p, MID)
        body(b * PAIRS + (PAIRS - 1), b, PAIRS - 1, LAST)
    with eng.Fori(0, PAIRS - 1) as p:
        body(p + (B - 1) * PAIRS, B - 1, p, MID)
    body(B * PAIRS - 1, B - 1, PAIRS - 1, FINAL)


def phase1(nc, xT, wqkv, bqkv, ropeT, od, rd):
    fp32, f32r = mybir.dt.float32, mybir.dt.float32r
    ALU, ACT, AX = mybir.AluOpType, mybir.ActivationFunctionType, mybir.AxisListType

    x_v = xT.rearrange("b (p t) n -> b t p n", t=CT)
    w_v = wqkv.rearrange("s o (p t) n -> s o p (t n)", t=CT)

    with ExitStack() as ctx:
        def sb(name, shape, dt=fp32):
            return ctx.enter_context(nc.sbuf_tensor(name, shape, dt))

        def ps(name, shape):
            return ctx.enter_context(nc.psum_tensor(name, shape, fp32))

        def sem(name):
            return ctx.enter_context(nc.semaphore(name))

        xn_hi, xn_lo = sb("xn_hi", [P, CT, N], f32r), sb("xn_lo", [P, CT, N], f32r)
        xs = sb("xs", [P, 2, N])
        w_raw = sb("w_raw", [P, CT * P])
        w_hi, w_lo = sb("w_hi", [P, 2, CT * P], f32r), sb("w_lo", [P, 2, CT * P], f32r)
        bias, bias_now = sb("bias", [P, PAIRS, 3]), sb("bias_now", [P, 3])
        sin2, cos2 = sb("sin2", [P, N]), sb("cos2", [P, N])
        raw = {"q": sb("raw_q", [P, N]), "k": sb("raw_k", [P, N]), "v": sb("raw_v", [P, N])}
        rot = sb("rot", [P, N])
        hi = {"q": sb("q_hi", [P, N], f32r), "k": sb("k_hi", [P, N], f32r)}
        lo = {"q": sb("q_lo", [P, N], f32r), "k": sb("k_lo", [P, N], f32r)}
        qa = [sb(f"qa{h}", [P, N], f32r) for h in range(2)]
        qb = [sb(f"qb{h}", [P, N], f32r) for h in range(2)]
        ka = [sb(f"ka{h}", [P, N], f32r) for h in range(2)]
        kb = [sb(f"kb{h}", [P, N], f32r) for h in range(2)]
        vs = [sb(f"vs{h}", [P, KT, 3 * D], f32r) for h in range(2)]
        p_hi, p_lo = sb("p_hi", [P, 4, 2, Q], f32r), sb("p_lo", [P, 2, 2, Q], f32r)
        acc, acc_sum = sb("acc", [P, 2, Q]), sb("acc_sum", [P, Q])
        t1 = sb("t1", [D, Q])
        numer, recip_b = sb("numer", [P, N]), sb("recip_b", [P, N])
        rows = sb("rows", [P, N])
        cols, cols_inv = sb("cols", [P, 2, KT]), sb("cols_inv", [P, KT])
        maxes, neg_m = sb("maxes", [P, 4, 2]), sb("neg_m", [P, 4], f32r)
        ident, ident_r = sb("ident", [P, P]), sb("ident_r", [P, P], f32r)
        ones = sb("ones", [P, P])
        group = sb("group", [P, P])
        stats, mv = sb("stats", [P, 2 * CT, 6]), sb("mv", [P, 2])
        gmean, gdev, gvar, rstd = sb("gmean", [P, 1]), sb("gdev", [P, 2]), sb("gvar", [P, 1]), sb("rstd", [P, 1])
        minus_half = sb("minus_half", [P, 1])

        st = ps("st", [P, 2, 2, Q])
        u1, u2 = ps("u1", [P, Q]), ps("u2", [P, Q])
        bx, by = ps("bx", [P, Q]), ps("by", [P, Q])

        dve_setup, pool_setup = sem("dve_setup"), sem("pool_setup")
        consts_dma = sem("consts_dma")
        st_done = sem("st_done")
        hi_done = sem("hi_done")
        exp_done = sem("exp_done")
        lo_done = sem("lo_done")
        pv_done = sem("pv_done")
        acc_done = sem("acc_done")
        fold_done = sem("fold_done")
        y_done = sem("y_done")
        y_free = sem("y_free")
        x_done = sem("x_done")
        bias_done = sem("bias_done")
        x_free = sem("x_free")
        w_load = sem("w_load")
        whi_done, wlo_done = sem("whi_done"), sem("wlo_done")
        rot_load = {o: sem(f"rot_{o}_load") for o in "qk"}
        mul_done = sem("mul_done")
        mul1_done = sem("mul1_done")
        add_done = sem("add_done")
        qkhi_done, qklo_done = sem("qkhi_done"), sem("qklo_done")
        set_load = [sem("set0_load"), sem("set1_load")]
        vhi_done = sem("vhi_done")
        negm_done = sem("negm_done")
        t1_done = sem("t1_done")
        t2_done = sem("t2_done")
        u_free = sem("u_free")
        lorow_done = sem("lorow_done")
        cols_load = sem("cols_load")
        colsum_done = sem("colsum_done")
        recip_done = sem("recip_done")
        rd_store = sem("rd_store")
        rb_load = sem("rb_load")
        out_done = sem("out_done")
        od_store = sem("od_store")
        xst_load = sem("xst_load")
        xst_done = sem("xst_done")
        xn_load = [sem("xn_load0"), sem("xn_load1")]
        xnorm_done = sem("xnorm_done")
        xhi_done, xlo_done = sem("xhi_done"), sem("xlo_done")
        gn_dve, gn_pe, gn_pool = sem("gn_dve"), sem("gn_pe"), sem("gn_pool")

        def x_count(it, job):
            return it * len(X_JOBS) + X_FIRST + X_JOBS.index(job) + 1

        def y_count(it, n):
            return it * Y_JOBS + Y_FIRST + n + 1

        def w_job(it, o):
            return it * 3 + {"k": 4, "v": 5, "q": 6}[o]

        def x_taken(it, job):
            return x_count(it, job) + 1

        def y_taken(it, n):
            return y_count(it, n) + 1

        W_BUF = {"q": 0, "k": 1, "v": 0}

        block = ctx.enter_context(nc.Block())

        @block.sync
        def _(sp):
            def load_w(job, slot, o):
                job, slot = ahead(sp, job, slot)
                if not (isinstance(job, int) and job == 0):
                    sp.wait_ge(wlo_done, job)
                sp.dma_start(w_raw[:], w_v[bass.ds(slot, 1), "qkv".index(o)]).then_inc(w_load, 16)

            def load_norm_tile(b, t):
                b, split = ahead(sp, b, b * CT + (t - 1))
                if t >= 2:
                    sp.wait_ge(xlo_done, split)
                sp.dma_start(xs[:, t % 2, :], x_v[bass.ds(b, 1), t]).then_inc(xn_load[t % 2], 16)

            def rotate(e, o):
                taken, used = ahead(sp, x_taken(e - 1, (o, 1)), e * 2 + "qk".index(o))
                sp.wait_ge(x_free, taken)
                if not (isinstance(used, int) and used == 0):
                    sp.wait_ge(add_done, used)
                for to, src in ((0, 32), (32, 0), (64, 96), (96, 64)):
                    sp.dma_start(rot[to:to + 32, :], raw[o][src:src + 32, :]).then_inc(rot_load[o], 16)

            def spread(split, h, *parts):
                sp.wait_ge(qklo_done, split)
                rows_h = slice(h * D, h * D + D)
                copies = {"q": ((qa[h][0:D, :], hi["q"]), (qa[h][D:P, :], lo["q"]), (qb[h][0:D, :], hi["q"])),
                          "k": ((ka[h][0:D, :], hi["k"]), (ka[h][D:P, :], hi["k"]), (kb[h][0:D, :], lo["k"]))}
                for o in parts:
                    for dst, src in copies[o]:
                        sp.dma_start(dst.bitcast(fp32), src[rows_h, :].bitcast(fp32)).then_inc(set_load[h], 16)

            def sums_to_columns(it, h, taken):
                lo_rows, taken = ahead(sp, it * 4 + (3 if h == 0 else 1), taken)
                sp.wait_ge(lorow_done, lo_rows)
                sp.wait_ge(y_free, taken)
                sp.dma_start(cols[:, 0, :], rows[0:1, :]).then_inc(cols_load, 16)
                sp.dma_start(cols[:, 1, :], rows[D:D + 1, :]).then_inc(cols_load, 16)

            def spread_reciprocals(it, h):
                recips, stored, outputs = ahead(sp, it * 2 + (2 if h == 0 else 1),
                                                it * 32 + (32 if h == 0 else 16), it * 32 + 16)
                sp.wait_ge(recip_done, recips)
                sp.dma_start(rd.rearrange("(p j) -> p j", j=KT), cols_inv[:]).then_inc(rd_store, 16)
                sp.wait_ge(rd_store, stored)
                if h == 0:
                    sp.wait_ge(od_store, outputs)
                sp.dma_start(recip_b[h * D:h * D + D, :],
                             rd.rearrange("(o n) -> o n", o=1).to_broadcast([D, N])).then_inc(rb_load, 16)

            def store_output(it, h):
                slot, outputs = ahead(sp, it + 1 if h == 0 else it, it * 2 + (3 if h == 0 else 2))
                sp.wait_ge(out_done, outputs)
                sp.dma_start(od[bass.ds(slot, 1), h * D:h * D + D, :],
                             recip_b[h * D:h * D + D, :]).then_inc(od_store, 16)

            for h in range(2):
                sp.dma_start(sin2[h * D:h * D + D, :], ropeT[0:D, :]).then_inc(consts_dma, 16)
                sp.dma_start(cos2[h * D:h * D + D, :], ropeT[D:2 * D, :]).then_inc(consts_dma, 16)
            sp.dma_start(bias[:].rearrange("p a o -> p (a o)"), bqkv).then_inc(consts_dma, 16)
            for t in range(CT):
                if t:
                    sp.wait_ge(xst_done, t)
                sp.dma_start(xs[:, 0, :], x_v[0, t]).then_inc(xst_load, 16)
            load_w(0, 0, "q")
            sp.wait_ge(xst_done, CT)
            load_norm_tile(0, 0)
            load_norm_tile(0, 1)
            load_w(1, 0, "k")
            for t in range(2, CT):
                load_norm_tile(0, t)
            load_w(2, 0, "v")
            rotate(0, "q")
            rotate(0, "k")
            spread(2, 0, "q", "k")
            load_w(3, 1, "q")

            def body(it, b, p, kind):
                e = it + 1
                nxt = kind != FINAL
                Y = y_index(kind)
                norm = kind == LAST
                old, split = ahead(sp, it * STEPS + 1, it * 2 + 2)
                sp.wait_ge(st_done, old)
                spread(split, 1, "q", "k")
                if nxt:
                    if not (isinstance(b, int) and b == B - 1):
                        used, normed, nb = ahead(sp, it + CT, b * CT + CT, b + 1)
                        sp.wait_ge(xst_done, used)
                        sp.wait_ge(xlo_done, normed)
                        sp.dma_start(xs[:, 0, :], x_v[bass.ds(nb, 1), bass.ds(p, 1)]).then_inc(xst_load, 16)
                    if norm:
                        used, _ = ahead(sp, it + (CT + 1), w_job(it, "k"))
                        sp.wait_ge(xst_done, used)
                    load_w(w_job(it, "k"), (p + 1) % PAIRS if norm else p + 1, "k")
                if norm:
                    for t in range(CT):
                        load_norm_tile(b + 1, t)
                sums_to_columns(it, 1, y_taken(it, Y[("sum", -1)]))
                if nxt:
                    load_w(w_job(it, "v"), (p + 1) % PAIRS if norm else p + 1, "v")
                if kind == MID:
                    rotate(e, "q")
                spread_reciprocals(it, 1)
                if kind == LAST:
                    rotate(e, "q")
                if nxt:
                    load_w(w_job(it, "q"), p + 2, "q")
                    rotate(e, "k")
                store_output(it, 1)
                if nxt:
                    old, q_split = ahead(sp, it * STEPS + (STEPS // 2 + 1), e * 2 + 1)
                    sp.wait_ge(st_done, old)
                    spread(q_split, 0, "q")
                    k_split, _ = ahead(sp, e * 2 + 2, 0)
                    spread(k_split, 0, "k")
                sums_to_columns(it, 0, y_taken(it, Y[("sum", 1)]))
                spread_reciprocals(it, 0)
                store_output(it, 0)

            each_iteration(sp, body)
            it = B * PAIRS
            sums_to_columns(it, 1, y_taken(it - 1, Y_LAST))
            spread_reciprocals(it, 1)
            store_output(it, 1)
            sp.wait_ge(od_store, it * 32 + 16)

        @block.gpsimd
        def _(pool):
            g = nc.gpsimd
            g.memset(ident[:], 0.0).then_inc(pool_setup, 1)
            g.memset(group[:], 1.0 / GROUP_P).then_inc(pool_setup, 1)
            g.memset(minus_half[:], -0.5).then_inc(pool_setup, 1)
            g.memset(acc_sum[:], 1.0).then_inc(fold_done, 1)
            g.memset(rows[:], 1.0).then_inc(acc_done, 3)
            g.memset(numer[:], 1.0).then_inc(out_done, 1)
            pool.wait_ge(pool_setup, 3)
            g.affine_select(out=ident[:], in_=ident[:], compare_op=ALU.not_equal, fill=1.0, base=0,
                            pattern=[[-1, P]], channel_multiplier=1).then_inc(pool_setup, 1)
            gv = group[:].rearrange("p (g j) -> p g j", j=GROUP_P)
            g.affine_select(out=gv, in_=gv, compare_op=ALU.is_ge, fill=0.0, base=0,
                            pattern=[[-GROUP_P, P // GROUP_P], [0, GROUP_P]],
                            channel_multiplier=1).then_inc(pool_setup, 1)
            pool.wait_ge(pool_setup, 5)
            g.affine_select(out=gv, in_=gv, compare_op=ALU.is_ge, fill=0.0, base=GROUP_P - 1,
                            pattern=[[GROUP_P, P // GROUP_P], [0, GROUP_P]],
                            channel_multiplier=-1).then_inc(pool_setup, 1)

            def split_w(job, o, free):
                pool.wait_ge(whi_done, job + 1)
                if free is not None:
                    pool.wait_ge(x_done, free)
                g.tensor_tensor(w_lo[:, W_BUF[o], :], w_raw[:], w_hi[:, W_BUF[o], :],
                                ALU.subtract).then_inc(wlo_done, 1)

            def rope(e, o):
                pool.wait_ge(rot_load[o], e * 64 + 64)
                g.tensor_tensor(raw[o][:], raw[o][:], cos2[:], ALU.mult).then_inc(mul1_done, 1)
                g.tensor_tensor(rot[:], rot[:], sin2[:], ALU.mult).then_inc(mul_done, 1)

            def add_up(it, s, Y):
                u, r = divmod(s, 4)
                if r == 0:
                    return
                pool.wait_ge(hi_done, it * STEPS + s + 1)
                if r == 1:
                    pool.wait_ge(fold_done, it * 4 + u + 1)
                    g.tensor_tensor(acc[:], p_hi[:, 0], p_hi[:, 1], ALU.add).then_inc(acc_done, 1)
                else:
                    pool.wait_ge(acc_done, it * 12 + 3 * u + r + 2)
                    g.tensor_tensor(acc[:], acc[:], p_hi[:, r], ALU.add).then_inc(acc_done, 1)
                if r == 3:
                    pool.wait_ge(acc_done, it * 12 + 3 * u + 6)
                    pool.wait_ge(y_done, y_count(it, Y[("sum", u - 1)]))
                    g.tensor_tensor(acc_sum[:], acc[:, 0], acc[:, 1], ALU.add).then_inc(fold_done, 1)

            def normalise(it, h, folds=None):
                if h == 1:
                    pool.wait_ge(fold_done, folds)
                pool.wait_ge(rb_load, it * 32 + (32 if h == 0 else 16))
                pool.wait_ge(u_free, it * 4 + (3 if h == 0 else 1))
                part = slice(h * D, h * D + D)
                g.tensor_tensor(recip_b[part, :], numer[part, :], recip_b[part, :],
                                ALU.mult).then_inc(out_done, 1)
                if h == 1:
                    pool.wait_ge(out_done, it * 2 + 2)

            def group_rstd(b):
                pool.wait_ge(gn_dve, b * 5 + 5)
                g.tensor_tensor(rstd[:], gvar[:], minus_half[:], ALU.pow).then_inc(gn_pool, 1)

            group_rstd(0)
            split_w(0, "q", None)
            split_w(1, "k", None)
            split_w(2, "v", 2)
            rope(0, "q")
            rope(0, "k")
            split_w(3, "q", 6)

            def body(it, b, p, kind):
                Y = y_index(kind)
                nxt = kind != FINAL
                for s in range(STEPS):
                    if s == 0 and kind == LAST:
                        group_rstd(b + 1)
                    if nxt and s == 8:
                        rope(it + 1, "k")
                    if s + 1 < STEPS:
                        add_up(it, s + 1, Y)
                    if nxt and s == 2:
                        split_w(w_job(it, "k"), "k", it * 8 + 4)
                    if nxt and s == (5 if kind == MID else 7):
                        rope(it + 1, "q")
                    if s == 6:
                        normalise(it, 1, it * 4 + 3)
                    if nxt and s == (4 if kind == MID else 6):
                        split_w(w_job(it, "v"), "v", x_count(it, ("q", 1)))
                    if s == 14:
                        normalise(it, 0)
                    if nxt and s == 14:
                        split_w(w_job(it, "q"), "q", x_count(it, ("v", 1)))

            each_iteration(pool, body)
            normalise(B * PAIRS, 1, B * PAIRS * 4 + 1)

        @block.scalar
        def _(act):
            a = nc.scalar

            def split_w(job, o, free):
                act.wait_ge(w_load, job * 16 + 16)
                if free is not None:
                    act.wait_ge(x_done, free)
                a.copy(w_hi[:, W_BUF[o], :], w_raw[:]).then_inc(whi_done, 1)

            def exps(it, s):
                u, r = divmod(s, 4)
                act.wait_ge(st_done, it * STEPS + s + 2)
                act.wait_ge(pv_done, it * STEPS + s + 1)
                act.wait_ge(acc_done, it * 12 + 3 * u + max(r, 1))
                a.activation(p_hi[:, r], st[:, s % 2], ACT.Exp, scale=SCALE).then_inc(hi_done, 1)
                a.activation(st[:, s % 2], st[:, s % 2], ACT.Exp, scale=SCALE).then_inc(exp_done, 1)

            def evacuate(e, count, o, half):
                act.wait_ge(bias_done, e + 1)
                if o != "v" and half == 0 and not (isinstance(e, int) and e == 0):
                    act.wait_ge(qklo_done, e * 2 + ("qk".index(o) - 1))
                act.wait_ge(x_done, count)
                n = "qkv".index(o)
                a.activation(raw[o][:, half * Q:half * Q + Q], bx[:], ACT.Identity,
                             bias=bias_now[:, n:n + 1]).then_inc(x_free, 1)

            def round_qk(e, o):
                n = "qk".index(o)
                act.wait_ge(add_done, e * 2 + n + 1)
                if not (isinstance(e, int) and e == 0):
                    act.wait_ge(set_load[1], e * 96)
                a.copy(hi[o][:], raw[o][:]).then_inc(qkhi_done, 1)

            def v_hi(e, h, count, free):
                act.wait_ge(x_done, count)
                if free is not None:
                    act.wait_ge(pv_done, free)
                a.copy(vs[h][:, :, D:2 * D], bx[:].rearrange("p (t d) -> p t d", d=D)).then_inc(vhi_done, 1)

            def minus_max_row(e, h, half, count):
                act.wait_ge(y_done, count)
                a.copy(qb[h][D:D + 1, half * Q:half * Q + Q], by[D:D + 1, :]).then_inc(y_free, 1)

            def hi_sum_row(it, u, count):
                act.wait_ge(y_done, count)
                if u == 0:
                    act.wait_ge(cols_load, it * 64 + 32)
                elif u == 2:
                    act.wait_ge(cols_load, it * 64 + 64)
                half = u % 2
                a.copy(rows[0:1, half * Q:half * Q + Q], by[0:1, :]).then_inc(y_free, 1)

            def unit_out(it, u):
                act.wait_ge(pv_done, it * STEPS + 4 * u + 8)
                act.wait_ge(u_free, it * 4 + u + 1)
                a.copy(t1[:], u1[D:P, :]).then_inc(t1_done, 1)
                if u == 0:
                    act.wait_ge(cols_load, it * 64 + 32)
                elif u == 2:
                    act.wait_ge(cols_load, it * 64 + 64)
                half = u % 2
                a.copy(rows[D:D + 1, half * Q:half * Q + Q], u2[D:D + 1, :]).then_inc(lorow_done, 1)

            def round_x(b, t):
                act.wait_ge(xnorm_done, b * CT + t + 1)
                a.copy(xn_hi[:, t, :], xs[:, t % 2, :]).then_inc(xhi_done, 1)

            act.wait_ge(consts_dma, 80)
            act.wait_ge(dve_setup, DVE_SETUP)
            act.wait_ge(pool_setup, POOL_SETUP)
            split_w(0, "q", None)
            for t in range(CT):
                round_x(0, t)
            split_w(1, "k", None)
            evacuate(0, 1, "q", 0)
            evacuate(0, 2, "q", 1)
            split_w(2, "v", 2)
            evacuate(0, 3, "k", 0)
            evacuate(0, 4, "k", 1)
            round_qk(0, "q")
            evacuate(0, 5, "v", 0)
            evacuate(0, 6, "v", 1)
            round_qk(0, "k")
            v_hi(0, 0, 7, None)
            split_w(3, "q", 6)
            minus_max_row(0, 0, 0, Y_FIRST - 2)
            exps(0, 0)

            def body(it, b, p, kind):
                Y, plan = y_index(kind), y_plan(kind)
                nxt = kind != FINAL
                e = it + 1
                for s in range(STEPS):
                    if s == 0:
                        v_hi(it, 1, x_count(it, ("tr", 1)), it * STEPS + 4)
                    if s < STEPS - 1 or nxt:
                        exps(it, s + 1)
                    if nxt and s == 14:
                        split_w(w_job(it, "q"), "q", x_count(it, ("v", 1)))
                    ended = EVAC[kind].get(s)
                    early = ended and ended not in [job[:2] for job in X_PLAN[kind][s][1]]
                    if early:
                        evacuate(e, x_count(it, ended), *ended)
                    if nxt and s == (7 if kind == MID else 8):
                        round_qk(e, "q")
                    if nxt and s == 9:
                        round_qk(e, "k")
                    for j in [j for place in plan[s] for j in place]:
                        if j[0] == "row":
                            minus_max_row(e if j[-1] else it, j[1], j[2], y_count(it, Y[j]))
                        elif j[0] == "sum":
                            hi_sum_row(it, j[1], y_count(it, Y[j]))
                    if kind == LAST and 1 <= s <= 3:
                        round_x(b + 1, 2 * (s - 1))
                        round_x(b + 1, 2 * (s - 1) + 1)
                    if s % 4 == 3:
                        unit_out(it, s // 4)
                    if ended and not early:
                        evacuate(e, x_count(it, ended), *ended)
                    if nxt and s == 2:
                        split_w(w_job(it, "k"), "k", it * 8 + 4)
                    if nxt and s == (4 if kind == MID else 6):
                        split_w(w_job(it, "v"), "v", x_count(it, ("q", 1)))
                    if nxt and s == 14:
                        v_hi(e, 0, x_count(it, ("tr", 0)), it * STEPS + 12)

            each_iteration(act, body)
            hi_sum_row(B * PAIRS, -1, y_count(B * PAIRS - 1, Y_LAST))

        @block.vector
        def _(dve):
            v = nc.vector

            def tile_stats(n, k):
                dve.wait_ge(xst_load, n * 16 + 16)
                v.bn_stats(stats[:, bass.ds(k * 2, 1), :], xs[:, 0, 0:Q])
                v.bn_stats(stats[:, bass.ds(k * 2 + 1, 1), :], xs[:, 0, Q:N]).then_inc(xst_done, 1)

            def group_stats(b, n):
                dve.wait_ge(xst_done, n)
                v.memset(gdev[:], 0.0)
                v.bn_aggr(mv[:], stats[:].rearrange("p k s -> p (k s)")).then_inc(gn_dve, 1)
                dve.wait_ge(gn_pe, b * 2 + 1)
                v.tensor_copy(gmean[:], bx[:, 0:1]).then_inc(gn_dve, 1)
                dve.wait_ge(gn_dve, b * 5 + 2)
                v.tensor_tensor(gdev[:, 0:1], mv[:, 0:1], gmean[:], ALU.subtract).then_inc(gn_dve, 1)
                dve.wait_ge(gn_dve, b * 5 + 3)
                v.scalar_tensor_tensor(gdev[:, 1:2], gdev[:, 0:1], gdev[:, 0:1], mv[:, 1:2],
                                       ALU.mult, ALU.add).then_inc(gn_dve, 1)
                dve.wait_ge(gn_pe, b * 2 + 2)
                v.tensor_scalar(gvar[:], bx[:, 2:3], EPS, None, ALU.add).then_inc(gn_dve, 1)
                dve.wait_ge(gn_pool, b + 1)

            def norm_tile(b, t):
                dve.wait_ge(xn_load[t % 2], b * 48 + 16 * (t // 2) + 16)
                v.tensor_scalar(xs[:, t % 2, :], xs[:, t % 2, :], gmean[:], rstd[:],
                                ALU.subtract, ALU.mult).then_inc(xnorm_done, 1)

            def x_lo(b, t):
                dve.wait_ge(xhi_done, b * CT + t + 1)
                v.tensor_tensor(xn_lo[:, t, :], xs[:, t % 2, :], xn_hi[:, t, :],
                                ALU.subtract).then_inc(xlo_done, 1)

            def pair_bias(pair):
                v.tensor_copy(bias_now[:], bias[:, bass.ds(pair, 1), :]).then_inc(bias_done, 1)

            def p_low(it, s):
                dve.wait_ge(exp_done, it * STEPS + s + 1)
                dve.wait_ge(pv_done, it * STEPS + s + 3)
                v.tensor_tensor(p_lo[:, s % 2], st[:, s % 2], p_hi[:, s % 4],
                                ALU.subtract).then_inc(lo_done, 1)

            def rope_add(e, o):
                n = "qk".index(o)
                dve.wait_ge(mul1_done, e * 2 + n + 1)
                dve.wait_ge(mul_done, e * 2 + n + 1)
                v.tensor_tensor(raw[o][:], raw[o][:], rot[:], ALU.add).then_inc(add_done, 1)

            def qk_lo(e, o):
                n = "qk".index(o)
                dve.wait_ge(qkhi_done, e * 2 + n + 1)
                v.tensor_tensor(lo[o][:], raw[o][:], hi[o][:], ALU.subtract).then_inc(qklo_done, 1)

            def v_lo(e, h):
                dve.wait_ge(vhi_done, e * 2 + h + 1)
                v.tensor_tensor(vs[h][:, :, 0:D], bx[:].rearrange("p (t d) -> p t d", d=D),
                                vs[h][:, :, D:2 * D], ALU.subtract).then_inc(x_free, 1)

            def maximum(count, i):
                dve.wait_ge(y_done, count)
                v.tensor_reduce(maxes[:, i // 2, i % 2:i % 2 + 1], by[:], AX.X, ALU.max,
                                negate=True).then_inc(y_free, 1)
                if i == 7:
                    dve.wait_ge(y_free, count + 1)
                    v.tensor_tensor(neg_m[:], maxes[:, :, 0], maxes[:, :, 1], ALU.min).then_inc(negm_done, 1)

            def unit_sum(it, u):
                h, half = divmod(u, 2)
                dve.wait_ge(t1_done, it * 4 + u + 1)
                v.tensor_tensor(t1[:], u1[0:D, :], t1[:], ALU.add).then_inc(t2_done, 1)
                dve.wait_ge(t2_done, it * 4 + u + 1)
                if u == 0:
                    dve.wait_ge(out_done, it * 2 + 1)
                elif u == 2:
                    dve.wait_ge(out_done, it * 2 + 2)
                v.tensor_tensor(numer[h * D:h * D + D, half * Q:half * Q + Q], u2[0:D, :], t1[:],
                                ALU.add).then_inc(u_free, 1)

            def reciprocals(it, h):
                n = it * 2 + (2 if h == 0 else 1)
                dve.wait_ge(cols_load, it * 64 + (64 if h == 0 else 32))
                v.tensor_tensor(cols[:, 0, :], cols[:, 0, :], cols[:, 1, :], ALU.add).then_inc(colsum_done, 1)
                dve.wait_ge(colsum_done, n)
                v.reciprocal(cols_inv[:], cols[:, 0, :]).then_inc(recip_done, 1)

            v.memset(ones[:], 1.0).then_inc(dve_setup, 1)
            for h in range(2):
                v.memset(vs[h][:, :, 2 * D:3 * D].bitcast(fp32), 1.0).then_inc(dve_setup, 1)
                v.memset(kb[h][D:D + 1, :].bitcast(fp32), 1.0).then_inc(dve_setup, 1)
            v.memset(recip_b[0:1, 0:1], 1.0).then_inc(st_done, 1)
            v.memset(recip_b[0:1, 1:2], 1.0).then_inc(lo_done, 2)
            v.memset(recip_b[0:1, 2:3], 1.0).then_inc(pv_done, 4)
            v.memset(recip_b[0:1, 3:4], 1.0).then_inc(y_free, 1)
            v.memset(recip_b[0:1, 4:5], 1.0).then_inc(x_free, 1)
            v.memset(recip_b[0:1, 5:6], 1.0).then_inc(u_free, 1)
            v.memset(recip_b[0:1, 6:7], 1.0).then_inc(lorow_done, 1)
            dve.wait_ge(pool_setup, POOL_SETUP)
            v.tensor_copy(ident_r[:], ident[:]).then_inc(dve_setup, 1)
            dve.wait_ge(consts_dma, 80)
            for h in range(2):
                v.tensor_scalar(sin2[h * D:h * D + 32, :], sin2[h * D:h * D + 32, :], -1.0, None,
                                ALU.mult).then_inc(dve_setup, 1)
            pair_bias(0)
            for t in range(CT):
                tile_stats(t, t)
            group_stats(0, CT)
            for t in range(CT):
                norm_tile(0, t)
                if t >= 1:
                    x_lo(0, t - 1)
            x_lo(0, CT - 1)
            rope_add(0, "q")
            qk_lo(0, "q")
            rope_add(0, "k")
            qk_lo(0, "k")
            v_lo(0, 0)
            for i in range(8):
                maximum(i + 1, i)
            p_low(0, 0)
            for i in range(2):
                maximum(Y_FIRST - 1 + i, i)

            def body(it, b, p, kind):
                Y, plan = y_index(kind), y_plan(kind)
                nxt = kind != FINAL
                e = it + 1

                def maxima(jobs):
                    for j in jobs:
                        if j[0] == "max":
                            maximum(y_count(it, Y[j]), j[3])

                for s in range(STEPS):
                    maxima(plan[s][0])
                    if s == 0:
                        v_lo(it, 1)
                    if nxt and s == 9:
                        rope_add(e, "k")
                    maxima(plan[s][1])
                    if s < STEPS - 1 or nxt:
                        p_low(it, s + 1)
                    maxima(plan[s][2] + plan[s][3])
                    if nxt and s == 8:
                        qk_lo(e, "q")
                    if nxt and s == 9:
                        qk_lo(e, "k")
                    if nxt and s == 0:
                        pair_bias(p + 1 if kind == MID else 0)
                    if kind == LAST and s == 0:
                        tile_stats(it + CT, CT - 1)
                        group_stats(b + 1, it + (CT + 1))
                    if kind == LAST and 1 <= s <= 3:
                        for t in (2 * s - 2, 2 * s - 1):
                            norm_tile(b + 1, t)
                        for t in (2 * s - 2, 2 * s - 1):
                            x_lo(b + 1, t)
                    if s == 4:
                        reciprocals(it, 1)
                    if kind == MID and s == 10 and not (isinstance(b, int) and b == B - 1):
                        tile_stats(it + CT, p)
                    if s == 13:
                        reciprocals(it, 0)
                    if s % 4 == 3:
                        unit_sum(it, s // 4)
                    if nxt and s == (6 if kind == MID else 7):
                        rope_add(e, "q")
                    if nxt and s == 14:
                        v_lo(e, 0)

            each_iteration(dve, body)
            reciprocals(B * PAIRS, 1)

        @block.tensor
        def _(pe):
            t_ = nc.tensor

            def project(e, o, half, first, last, xc, w):
                for i in range(first, last):
                    t, kind = divmod(i, 3)
                    if i == 0:
                        pe.wait_ge(x_free, xc)
                        pe.wait_ge(wlo_done, w + 1)
                    wt, xt = ((w_hi, xn_hi), (w_hi, xn_lo), (w_lo, xn_hi))[kind]
                    m = t_.matmul(bx[:], wt[:, W_BUF[o], t * P:t * P + P], xt[:, t, half * Q:half * Q + Q],
                                  start=i == 0, stop=i == PROD - 1)
                    if i == PROD - 1:
                        m.then_inc(x_done, 1)

            def transpose_v(h, xc):
                pe.wait_ge(x_free, xc)
                part = slice(h * D, h * D + D)
                t_.matmul(bx[:, 0:D], raw["v"][part, 0:P], ident[part, part], start=True, stop=True)
                for t in range(1, KT):
                    m = t_.transpose(bx[:, t * D:t * D + D], raw["v"][part, t * P:t * P + P], ident[part, part])
                m.then_inc(x_done, 1)

            def group_mean(b, xc):
                if xc is not None:
                    pe.wait_ge(x_free, xc)
                pe.wait_ge(gn_dve, b * 5 + 1)
                t_.matmul(bx[:, 0:1], group[:], mv[:, 0:1], start=True, stop=True).then_inc(gn_pe, 1)
                pe.wait_ge(gn_dve, b * 5 + 4)
                t_.matmul(bx[:, 2:3], group[:], gdev[:, 1:2], start=True, stop=True).then_inc(gn_pe, 1)

            def scores(it, s):
                h, half, kp = s // 8 % 2, s // 4 % 2, s % 4
                if s % 4 == 0:
                    pe.wait_ge(set_load[h], (it + s // STEPS) * 96 + 96)
                    if s % STEPS == 0:
                        pe.wait_ge(y_free, y_taken(it + s // STEPS - 1, ROW_0))
                    else:
                        pe.wait_ge(y_free, y_taken(it, y_index(MID)[("row", h, half, False)]))
                pe.wait_ge(lo_done, it * STEPS + s + 1)
                for j in range(2):
                    key = slice((2 * kp + j) * P, (2 * kp + j) * P + P)
                    qs = slice(half * Q, half * Q + Q)
                    t_.matmul(st[:, s % 2, j, :], ka[h][:, key], qa[h][:, qs], start=True, stop=False)
                    m = t_.matmul(st[:, s % 2, j, :], kb[h][0:D + 1, key], qb[h][0:D + 1, qs],
                                  start=False, stop=True)
                m.then_inc(st_done, 1)

            def values(it, s):
                u, kp = divmod(s, 4)
                h = u // 2
                if kp == 0:
                    if u == 0:
                        pe.wait_ge(x_free, x_taken(it - 1, ("tr", 0)))
                    elif u == 2:
                        pe.wait_ge(x_free, x_taken(it, ("tr", 1)))
                    pe.wait_ge(u_free, it * 4 + u + 1)
                    pe.wait_ge(lorow_done, it * 4 + u + 1)
                pe.wait_ge(hi_done, it * STEPS + s + 1)
                for j in range(2):
                    t_.matmul(u1[:], vs[h][:, 2 * kp + j, 0:2 * D], p_hi[:, s % 4, j, :],
                              start=kp == 0 and j == 0, stop=kp == 3 and j == 1)
                pe.wait_ge(lo_done, it * STEPS + s + 3)
                for j in range(2):
                    m = t_.matmul(u2[:], vs[h][:, 2 * kp + j, D:3 * D], p_lo[:, s % 2, j, :],
                                  start=kp == 0 and j == 0, stop=kp == 3 and j == 1)
                m.then_inc(pv_done, 1)

            def y_job(it, e, j, count):
                pe.wait_ge(y_free, count)
                if j[0] == "max":
                    _, h, half, i, _ = j
                    if i == 0 and half == 0:
                        pe.wait_ge(set_load[h], e * 96 + 96)
                    qt, kh = half * 4 + i // 2, i % 2
                    m = t_.matmul(by[:], qa[h][:, qt * P:qt * P + P], ka[h][:, kh * Q:kh * Q + Q],
                                  start=True, stop=True)
                elif j[0] == "row":
                    _, h, half, _ = j
                    pe.wait_ge(negm_done, e * 4 + 2 * h + half + 1)
                    for i in range(4):
                        m = t_.matmul(by[:, i * P:i * P + P], neg_m[:, i:i + 1].to_broadcast([P, P]),
                                      ident_r[:], start=True, stop=True)
                else:
                    pe.wait_ge(fold_done, it * 4 + j[1] + 2)
                    m = t_.matmul(by[:], ones[:], acc_sum[:], start=True, stop=True)
                m.then_inc(y_done, 1)

            pe.wait_ge(dve_setup, DVE_SETUP)
            pe.wait_ge(pool_setup, POOL_SETUP)
            group_mean(0, None)
            pe.wait_ge(xlo_done, CT)
            for n, (o, half) in enumerate([("q", 0), ("q", 1), ("k", 0), ("k", 1), ("v", 0), ("v", 1)]):
                project(0, o, half, 0, PROD, n + 1, n // 2)
            transpose_v(0, X_FIRST)
            for i in range(8):
                y_job(0, 0, ("max", 0, 0, i, False), i + 1)
            y_job(0, 0, ("row", 0, 0, False), Y_FIRST - 2)
            scores(0, 0)
            for i in range(2):
                y_job(0, 0, ("max", 0, 1, i, False), Y_FIRST - 1 + i)

            def body(it, b, p, kind):
                Y, plan = y_index(kind), y_plan(kind)
                e = it + 1
                done = {}

                def projections(s, part):
                    for o, half, n in X_PLAN[kind].get(s, ([], []))[part]:
                        i = done.get((o, half), 0)
                        if kind == LAST and (o, half, i) == ("q", 0, 0):
                            pe.wait_ge(xlo_done, b * CT + 2 * CT)
                        w = it * 3 + {"q": 3, "k": 4, "v": 5}[o]
                        project(e, o, half, i, i + n, x_count(it, (o, half)), w)
                        done[(o, half)] = i + n

                def y_jobs(jobs):
                    for j in jobs:
                        y_job(it, e if j[-1] is True else it, j, y_count(it, Y[j]))

                for s in range(STEPS):
                    if s == 0:
                        transpose_v(1, x_count(it, ("tr", 1)))
                    if s < STEPS - 1 or kind != FINAL:
                        scores(it, s + 1)
                    y_jobs(plan[s][0])
                    projections(s, 0)
                    if kind != FINAL and s == 14:
                        transpose_v(0, x_count(it, ("tr", 0)))
                    y_jobs(plan[s][1])
                    values(it, s)
                    y_jobs(plan[s][2])
                    projections(s, 1)
                    y_jobs(plan[s][3])
                    if kind == LAST and s == 0:
                        group_mean(b + 1, x_count(it, ("q", 0)))

            each_iteration(pe, body)
            last = B * PAIRS - 1
            y_job(last, last, ("sum", 3), y_count(last, Y_LAST))


def phase2(nc, xT, wp, bp, od, out):
    fp32, f32r = mybir.dt.float32, mybir.dt.float32r
    ALU = mybir.AluOpType
    wp_v = wp.rearrange("(t p) n -> p t n", p=P)
    x_v = xT.rearrange("b (t p) n -> b p t n", p=P)
    out_v = out.rearrange("b (t p) n -> b p t n", p=P)
    od_v = od.rearrange("s p n -> p s n")

    with ExitStack() as ctx:
        def sb(name, shape, dt=fp32):
            return ctx.enter_context(nc.sbuf_tensor(name, shape, dt))

        def sem(name):
            return ctx.enter_context(nc.semaphore(name))

        w_raw = sb("wp_raw", [P, CT, C])
        w_hi, w_lo = sb("wp_hi", [P, CT, C], f32r), sb("wp_lo", [P, CT, C], f32r)
        bias = sb("bias_p", [P, CT])
        att = [sb(f"att{h}", [P, CT, Q]) for h in range(2)]
        att_hi = [sb(f"att_hi{h}", [P, CT, Q], f32r) for h in range(2)]
        att_lo = [sb(f"att_lo{h}", [P, CT, Q], f32r) for h in range(2)]
        res = [sb(f"res{h}", [P, CT, Q]) for h in range(2)]
        banks = [ctx.enter_context(nc.psum_tensor(f"proj{c}", [P, Q], fp32)) for c in range(CT)]

        w_load, w_split = sem("wp_load"), sem("wp_split")
        att_load = [sem(f"att_load{h}") for h in range(2)]
        res_load = [sem(f"res_load{h}") for h in range(2)]
        out_store = [sem(f"out_store{h}") for h in range(2)]
        hi_done, lo_done = sem("att_hi_done"), sem("att_lo_done")
        proj_done, out_done = sem("proj_done"), sem("proj_out")

        block = ctx.enter_context(nc.Block())

        @block.sync
        def _(sp):
            sp.dma_start(w_raw[:], wp_v).then_inc(w_load, 16)
            sp.dma_start(bias[:], bp).then_inc(w_load, 16)

            def load(b, h, first):
                cols = slice(h * Q, h * Q + Q)
                b, slot, split, stored = ahead(sp, b, b * PAIRS + 1, b * 2 + (h - 1), b * 16)
                if not first:
                    sp.wait_ge(lo_done, split)
                sp.dma_start(att[h][:], od_v[:, bass.ds(slot, PAIRS), cols]).then_inc(att_load[h], 16)
                if not first:
                    sp.wait_ge(out_store[h], stored)
                sp.dma_start(res[h][:], x_v[bass.ds(b, 1), :, :, cols]).then_inc(res_load[h], 16)

            def store(b, h):
                b, done = ahead(sp, b, b * 12 + (6 * h + 6))
                sp.wait_ge(out_done, done)
                sp.dma_start(out_v[bass.ds(b, 1), :, :, h * Q:h * Q + Q], res[h][:]).then_inc(out_store[h], 16)

            load(0, 0, True)
            load(0, 1, True)
            with sp.Fori(0, B - 1) as b:
                for h in range(2):
                    store(b, h)
                    load(b + 1, h, False)
            for h in range(2):
                store(B - 1, h)
            for h in range(2):
                sp.wait_ge(out_store[h], B * 16)

        @block.scalar
        def _(act):
            act.wait_ge(w_load, 32)
            nc.scalar.copy(w_hi[:], w_raw[:]).then_inc(w_split, 1)

            def split(b, h, first):
                act.wait_ge(att_load[h], b * 16 + 16)
                if not first:
                    act.wait_ge(proj_done, b * 12 + (6 * h - 6))
                nc.scalar.copy(att_hi[h][:], att[h][:]).then_inc(hi_done, 1)

            for h in range(2):
                split(0, h, True)
            with act.Fori(1, B) as b:
                for h in range(2):
                    split(b, h, False)

        @block.vector
        def _(dve):
            dve.wait_ge(w_split, 1)
            nc.vector.tensor_tensor(w_lo[:], w_raw[:], w_hi[:], ALU.subtract).then_inc(w_split, 1)

            def split(b, h, first):
                dve.wait_ge(hi_done, b * 2 + h + 1)
                if not first:
                    dve.wait_ge(proj_done, b * 12 + (6 * h - 6))
                nc.vector.tensor_tensor(att_lo[h][:], att[h][:], att_hi[h][:], ALU.subtract).then_inc(lo_done, 1)

            def finish(b, h):
                dve.wait_ge(res_load[h], b * 16 + 16)
                for c in range(CT):
                    dve.wait_ge(proj_done, b * 12 + (6 * h + c + 1))
                    nc.vector.scalar_tensor_tensor(res[h][:, c, :], banks[c][:], bias[:, c:c + 1], res[h][:, c, :],
                                                   ALU.add, ALU.add).then_inc(out_done, 1)

            for h in range(2):
                split(0, h, True)
            with dve.Fori(0, B - 1) as b:
                for h in range(2):
                    finish(b, h)
                    split(b + 1, h, False)
            for h in range(2):
                finish(B - 1, h)

        @block.tensor
        def _(pe):
            pe.wait_ge(w_split, 2)

            def unit(b, h, first):
                pe.wait_ge(lo_done, b * 2 + h + 1)
                for c in range(CT):
                    if not first:
                        pe.wait_ge(out_done, b * 12 + (6 * h + c - 5))
                    for t in range(CT):
                        for w, a in ((w_hi, att_hi), (w_hi, att_lo), (w_lo, att_hi)):
                            m = nc.tensor.matmul(banks[c][:], w[:, t, c * P:c * P + P], a[h][:, t, :],
                                                 start=t == 0 and w is w_hi and a is att_hi,
                                                 stop=t == CT - 1 and w is w_lo)
                    m.then_inc(proj_done, 1)

            unit(0, 0, True)
            unit(0, 1, False)
            with pe.Fori(1, B) as b:
                for h in range(2):
                    unit(b, h, False)


def build(nc, xT, wqkv, bqkv, ropeT, wp, bp, out):
    fp32 = mybir.dt.float32
    od = nc.dram_tensor("attention_out", [B * PAIRS + 1, P, N], fp32, kind="Internal").ap()
    rd = nc.dram_tensor("reciprocals", [N], fp32, kind="Internal").ap()
    phase1(nc, xT, wqkv, bqkv, ropeT, od, rd)
    phase2(nc, xT, wp, bp, od, out)


def kernel(x, L0_conv_rope, L0_conv_qkv_w, L0_conv_qkv_b, L0_conv_proj_w, L0_conv_proj_b):
    import numpy as np
    import concourse.bacc as bacc
    from concourse.bass_utils import run_bass_kernel_spmd

    xT = np.ascontiguousarray(np.asarray(x).reshape(B, N, C).transpose(0, 2, 1))
    w = np.asarray(L0_conv_qkv_w).reshape(C, 3, PAIRS, P).transpose(2, 1, 0, 3)
    arrays = {
        "xT": xT,
        "wqkv": np.ascontiguousarray(np.concatenate([w, w[:2]], axis=0)),
        "bqkv": np.ascontiguousarray(np.asarray(L0_conv_qkv_b).reshape(3, PAIRS, P).transpose(2, 1, 0).reshape(P, -1)),
        "ropeT": np.ascontiguousarray(np.asarray(L0_conv_rope).T),
        "wp": np.ascontiguousarray(np.asarray(L0_conv_proj_w)),
        "bp": np.ascontiguousarray(np.asarray(L0_conv_proj_b).reshape(CT, P).T),
    }
    nc = bacc.Bacc("TRN2", target_bir_lowering=False, num_devices=1)
    args = [nc.dram_tensor(n, v.shape, mybir.dt.from_np(v.dtype), kind="ExternalInput").ap()
            for n, v in arrays.items()]
    out = nc.dram_tensor("yT", [B, C, N], mybir.dt.float32, kind="ExternalOutput").ap()
    build(nc, *args, out)
    r = run_bass_kernel_spmd(nc, [arrays], core_ids=[0])
    y = r.results[0]["yT"]
    return np.ascontiguousarray(y.transpose(0, 2, 1)).reshape(x.shape)
```

```python
from contextlib import ExitStack

import concourse.bass as bass
from concourse import mybir

B, N, C, H = 8, 1024, 768, 12
D = C // H
P = 128
CT = C // P
PAIRS = H // 2
GROUP = C // 32
GROUP_P = GROUP // CT
Q = 512
KT = N // P
STEPS = 2 * 2 * (KT // 2)
UNITS = 4
EPS = 1e-5
SCALE = float(D) ** -0.5
PROD = 3 * CT

MID, PRE, LAST, FINAL = "mid", "pre", "last", "final"

X_JOBS = [("tr", 1), ("q", 0), ("q", 1), ("k", 0), ("k", 1), ("v", 0), ("v", 1), ("tr", 0)]
X_FIRST = 7
V_PLAN = {8: ([("v", 0, 2)], [("v", 0, 3)]), 9: ([("v", 0, 4)], [("v", 0, 4)]), 10: ([("v", 0, 5)], []),
          11: ([("v", 1, 4)], [("v", 1, 3)]), 12: ([("v", 1, 3)], [("v", 1, 3)]),
          13: ([("v", 1, 3)], [("v", 1, 2)])}
MID_PLAN = {0: ([], [("q", 0, 8)]), 1: ([("q", 0, 5)], [("q", 0, 5)]),
            2: ([("q", 1, 5)], [("q", 1, 5)]), 3: ([("q", 1, 4)], [("q", 1, 4)]),
            4: ([("k", 0, 5)], [("k", 0, 5)]), 5: ([("k", 0, 4)], [("k", 0, 4)]),
            6: ([("k", 1, 6)], [("k", 1, 6)]), 7: ([("k", 1, 6)], []),
            **V_PLAN}
LAST_PLAN = {0: ([], [("q", 0, 6)]), 2: ([("q", 0, 3)], [("q", 0, 3)]), 4: ([("q", 0, 6)], [("q", 1, 9)]),
             5: ([("q", 1, 9)], [("k", 0, 9)]), 6: ([("k", 0, 9)], [("k", 1, 9)]), 7: ([("k", 1, 9)], []),
             **V_PLAN}
X_PLAN = {MID: MID_PLAN, PRE: MID_PLAN, LAST: LAST_PLAN, FINAL: {}}
EVAC_MID = {1: ("q", 0), 3: ("q", 1), 5: ("k", 0), 7: ("k", 1), 10: ("v", 0), 13: ("v", 1)}
EVAC_LAST = {4: ("q", 0), 5: ("q", 1), 6: ("k", 0), **{s: job for s, job in EVAC_MID.items() if s > 6}}
EVAC = {MID: EVAC_MID, PRE: EVAC_MID, LAST: EVAC_LAST, FINAL: {}}
NORM = {MID: {}, PRE: {14: (0, 1)}, LAST: {0: (2, 3), 2: (4, 5)}, FINAL: {}}
SPLIT = {MID: {}, PRE: {15: (0, 1)}, LAST: {1: (2, 3), 3: (4, 5)}, FINAL: {}}


def mx(head, half, i, nxt=False):
    return [("max", head, half, i, nxt)]


Y_PLAN = {
    0: ([], mx(0, 1, 2), mx(0, 1, 3), []),
    1: (mx(0, 1, 4), mx(0, 1, 5), mx(0, 1, 6), []),
    2: (mx(0, 1, 7), [("row", 0, 1, False)], [], [("sum", -1)]),
    3: (mx(1, 0, 0), mx(1, 0, 1), mx(1, 0, 2), []),
    4: (mx(1, 0, 3), mx(1, 0, 4), mx(1, 0, 5), []),
    5: (mx(1, 0, 6), mx(1, 0, 7), [("row", 1, 0, False)], []),
    6: ([("sum", 0)], [], mx(1, 1, 0), mx(1, 1, 1)),
    7: (mx(1, 1, 2), mx(1, 1, 3), [], []),
    8: (mx(1, 1, 4), mx(1, 1, 5), mx(1, 1, 6), []),
    9: (mx(1, 1, 7), [("row", 1, 1, False)], [], []),
    10: ([], [("sum", 1)], [], []),
    11: ([], [], mx(0, 0, 0, True), []),
    12: (mx(0, 0, 1, True), mx(0, 0, 2, True), mx(0, 0, 3, True), [("sum", 2)]),
    13: (mx(0, 0, 4, True), mx(0, 0, 5, True), mx(0, 0, 6, True), []),
    14: (mx(0, 0, 7, True), [("row", 0, 0, True)], [], []),
    15: (mx(0, 1, 0, True), [], mx(0, 1, 1, True), []),
}
Y_FIRST = 11


def y_plan(kind):
    keep = lambda jobs: [j for j in jobs if kind != FINAL or j[-1] is not True]
    return [tuple(keep(jobs) for jobs in Y_PLAN.get(s, ([], [], [], []))) for s in range(STEPS)]


def y_index(kind):
    order = [j for places in y_plan(kind) for jobs in places for j in jobs]
    return {j: n for n, j in enumerate(order)}


Y_JOBS = len(y_index(MID))
Y_LAST = len(y_index(FINAL))
ROW_0 = y_index(MID)[("row", 0, 0, True)]
POOL_SETUP, DVE_SETUP = 6, 8


def ahead(eng, *values):
    for value in values:
        if not isinstance(value, int):
            eng.to_reg(value)
    return values


def each_iteration(eng, body):
    with eng.Fori(0, B - 1) as b:
        with eng.Fori(0, PAIRS - 2) as p:
            body(b * PAIRS + p, b, p, MID)
        body(b * PAIRS + (PAIRS - 2), b, PAIRS - 2, PRE)
        body(b * PAIRS + (PAIRS - 1), b, PAIRS - 1, LAST)
    with eng.Fori(0, PAIRS - 1) as p:
        body(p + (B - 1) * PAIRS, B - 1, p, MID)
    body(B * PAIRS - 1, B - 1, PAIRS - 1, FINAL)


def phase1(nc, xT, wqkv, bqkv, ropeT, od, rd):
    fp32, f32r = mybir.dt.float32, mybir.dt.float32r
    ALU, ACT, AX = mybir.AluOpType, mybir.ActivationFunctionType, mybir.AxisListType

    x_v = xT.rearrange("b (p t) n -> b t p n", t=CT)
    w_v = wqkv.rearrange("s o (p t) n -> s o p (t n)", t=CT)

    with ExitStack() as ctx:
        def sb(name, shape, dt=fp32):
            return ctx.enter_context(nc.sbuf_tensor(name, shape, dt))

        def ps(name, shape):
            return ctx.enter_context(nc.psum_tensor(name, shape, fp32))

        def sem(name):
            return ctx.enter_context(nc.semaphore(name))

        xn_hi, xn_lo = sb("xn_hi", [P, CT, N], f32r), sb("xn_lo", [P, CT, N], f32r)
        xs = sb("xs", [P, 2, N])
        w_raw = sb("w_raw", [P, CT * P])
        w_hi, w_lo = sb("w_hi", [P, 2, CT * P], f32r), sb("w_lo", [P, 2, CT * P], f32r)
        bias, bias_now = sb("bias", [P, PAIRS, 3]), sb("bias_now", [P, 3])
        sin2, cos2 = sb("sin2", [P, N]), sb("cos2", [P, N])
        raw = {"q": sb("raw_q", [P, N]), "k": sb("raw_k", [P, N]), "v": sb("raw_v", [P, N])}
        rot = sb("rot", [P, N])
        hi = {"q": sb("q_hi", [P, N], f32r), "k": sb("k_hi", [P, N], f32r)}
        lo = {"q": sb("q_lo", [P, N], f32r), "k": sb("k_lo", [P, N], f32r)}
        qa = [sb(f"qa{h}", [P, N], f32r) for h in range(2)]
        qb = [sb(f"qb{h}", [P, N], f32r) for h in range(2)]
        ka = [sb(f"ka{h}", [P, N], f32r) for h in range(2)]
        kb = [sb(f"kb{h}", [P, N], f32r) for h in range(2)]
        vs = [sb(f"vs{h}", [P, KT, 3 * D], f32r) for h in range(2)]
        p_hi, p_lo = sb("p_hi", [P, 4, 2, Q], f32r), sb("p_lo", [P, 2, 2, Q], f32r)
        acc, acc_sum = sb("acc", [P, 2, Q]), sb("acc_sum", [P, Q])
        t1 = sb("t1", [D, Q])
        numer, recip_b = sb("numer", [P, N]), sb("recip_b", [P, N])
        rows = sb("rows", [P, N])
        cols, cols_inv = sb("cols", [P, 2, KT]), sb("cols_inv", [P, KT])
        maxes, neg_m = sb("maxes", [P, 4, 2]), sb("neg_m", [P, 4], f32r)
        ident, ident_r = sb("ident", [P, P]), sb("ident_r", [P, P], f32r)
        ones = sb("ones", [P, P])
        group = sb("group", [P, P])
        stats, mv = sb("stats", [P, 2 * CT, 6]), sb("mv", [P, 2])
        gmean, gdev, gvar, rstd = sb("gmean", [P, 1]), sb("gdev", [P, 2]), sb("gvar", [P, 1]), sb("rstd", [P, 1])
        minus_half = sb("minus_half", [P, 1])

        st = ps("st", [P, 2, 2, Q])
        u1, u2 = ps("u1", [P, Q]), ps("u2", [P, Q])
        bx, by = ps("bx", [P, Q]), ps("by", [P, Q])

        dve_setup, pool_setup = sem("dve_setup"), sem("pool_setup")
        consts_dma = sem("consts_dma")
        st_done = sem("st_done")
        hi_done = sem("hi_done")
        exp_done = sem("exp_done")
        lo_done = sem("lo_done")
        pv_done = sem("pv_done")
        acc_done = sem("acc_done")
        fold_done = sem("fold_done")
        y_done = sem("y_done")
        y_free = sem("y_free")
        x_done = sem("x_done")
        bias_done = sem("bias_done")
        x_free = sem("x_free")
        w_load = sem("w_load")
        whi_done, wlo_done = sem("whi_done"), sem("wlo_done")
        rot_load = {o: sem(f"rot_{o}_load") for o in "qk"}
        mul_done = sem("mul_done")
        mul1_done = sem("mul1_done")
        add_done = sem("add_done")
        qkhi_done, qklo_done = sem("qkhi_done"), sem("qklo_done")
        set_load = [sem("set0_load"), sem("set1_load")]
        vhi_done = sem("vhi_done")
        negm_done = sem("negm_done")
        t1_done = sem("t1_done")
        t2_done = sem("t2_done")
        u_free = sem("u_free")
        lorow_done = sem("lorow_done")
        cols_load = sem("cols_load")
        colsum_done = sem("colsum_done")
        recip_done = sem("recip_done")
        rd_store = sem("rd_store")
        rb_load = sem("rb_load")
        out_done = sem("out_done")
        od_store = sem("od_store")
        x0_load = [sem(f"x0_load{t}") for t in range(CT)]
        xst_load = sem("xst_load")
        xst_done = sem("xst_done")
        xn_load = [sem("xn_load0"), sem("xn_load1")]
        xnorm_done = sem("xnorm_done")
        xhi_done, xlo_done = sem("xhi_done"), sem("xlo_done")
        gn_dve, gn_pe, gn_pool = sem("gn_dve"), sem("gn_pe"), sem("gn_pool")

        def x_tile(b, t):
            if isinstance(b, int) and b == 0:
                return [raw["q"][:], raw["k"][:], raw["v"][:], rot[:], recip_b[:], xs[:, 0, :]][t]
            return xs[:, t % 2, :]

        def x_count(it, job):
            return it * len(X_JOBS) + X_FIRST + X_JOBS.index(job) + 1

        def y_count(it, n):
            return it * Y_JOBS + Y_FIRST + n + 1

        def w_job(it, o):
            return it * 3 + {"k": 4, "v": 5, "q": 6}[o]

        def x_taken(it, job):
            return x_count(it, job) + 1

        def y_taken(it, n):
            return y_count(it, n) + 1

        W_BUF = {"q": 0, "k": 1, "v": 0}

        block = ctx.enter_context(nc.Block())

        @block.sync
        def _(sp):
            def load_w(job, slot, o):
                job, slot = ahead(sp, job, slot)
                if not (isinstance(job, int) and job == 0):
                    sp.wait_ge(wlo_done, job)
                sp.dma_start(w_raw[:], w_v[bass.ds(slot, 1), "qkv".index(o)]).then_inc(w_load, 16)

            def load_norm_tile(b, t, stats_done=None):
                b, split = ahead(sp, b, b * CT + (t - 1))
                if stats_done is not None:
                    sp.wait_ge(xst_done, *ahead(sp, stats_done))
                if t >= 2:
                    sp.wait_ge(xlo_done, split)
                sp.dma_start(xs[:, t % 2, :], x_v[bass.ds(b, 1), t]).then_inc(xn_load[t % 2], 16)

            def rotate(e, o):
                taken, used = ahead(sp, x_taken(e - 1, (o, 1)), e * 2 + "qk".index(o))
                sp.wait_ge(x_free, taken)
                if not (isinstance(used, int) and used == 0):
                    sp.wait_ge(add_done, used)
                for to, src in ((0, 32), (32, 0), (64, 96), (96, 64)):
                    sp.dma_start(rot[to:to + 32, :], raw[o][src:src + 32, :]).then_inc(rot_load[o], 16)

            def spread(split, h, *parts):
                sp.wait_ge(qklo_done, split)
                rows_h = slice(h * D, h * D + D)
                copies = {"q": ((qa[h][0:D, :], hi["q"]), (qa[h][D:P, :], lo["q"]), (qb[h][0:D, :], hi["q"])),
                          "k": ((ka[h][0:D, :], hi["k"]), (ka[h][D:P, :], hi["k"]), (kb[h][0:D, :], lo["k"]))}
                for o in parts:
                    for dst, src in copies[o]:
                        sp.dma_start(dst.bitcast(fp32), src[rows_h, :].bitcast(fp32)).then_inc(set_load[h], 16)

            def sums_to_columns(it, h, taken):
                lo_rows, taken = ahead(sp, it * 4 + (3 if h == 0 else 1), taken)
                sp.wait_ge(lorow_done, lo_rows)
                sp.wait_ge(y_free, taken)
                sp.dma_start(cols[:, 0, :], rows[0:1, :]).then_inc(cols_load, 16)
                sp.dma_start(cols[:, 1, :], rows[D:D + 1, :]).then_inc(cols_load, 16)

            def spread_reciprocals(it, h):
                recips, stored, outputs = ahead(sp, it * 2 + (2 if h == 0 else 1),
                                                it * 32 + (32 if h == 0 else 16), it * 32 + 16)
                sp.wait_ge(recip_done, recips)
                sp.dma_start(rd.rearrange("(p j) -> p j", j=KT), cols_inv[:]).then_inc(rd_store, 16)
                sp.wait_ge(rd_store, stored)
                if h == 0:
                    sp.wait_ge(od_store, outputs)
                sp.dma_start(recip_b[h * D:h * D + D, :],
                             rd.rearrange("(o n) -> o n", o=1).to_broadcast([D, N])).then_inc(rb_load, 16)

            def store_output(it, h):
                slot, outputs = ahead(sp, it + 1 if h == 0 else it, it * 2 + (3 if h == 0 else 2))
                sp.wait_ge(out_done, outputs)
                sp.dma_start(od[bass.ds(slot, 1), h * D:h * D + D, :],
                             recip_b[h * D:h * D + D, :]).then_inc(od_store, 16)

            def load_first(t):
                sp.dma_start(x_tile(0, t), x_v[0, t]).then_inc(x0_load[t], 16)

            for t in range(CT // 2):
                load_first(t)
            for h in range(2):
                sp.dma_start(sin2[h * D:h * D + D, :], ropeT[0:D, :]).then_inc(consts_dma, 16)
                sp.dma_start(cos2[h * D:h * D + D, :], ropeT[D:2 * D, :]).then_inc(consts_dma, 16)
            sp.dma_start(bias[:].rearrange("p a o -> p (a o)"), bqkv).then_inc(consts_dma, 16)
            load_w(0, 0, "q")
            for t in range(CT // 2, CT):
                load_first(t)
            load_w(1, 0, "k")
            load_w(2, 0, "v")
            rotate(0, "q")
            rotate(0, "k")
            spread(2, 0, "q", "k")
            load_w(3, 1, "q")

            def body(it, b, p, kind):
                e = it + 1
                nxt = kind != FINAL
                Y = y_index(kind)
                slot = (p + 1) % PAIRS if kind == LAST else p + 1
                old, split = ahead(sp, it * STEPS + 1, it * 2 + 2)
                sp.wait_ge(st_done, old)
                spread(split, 1, "q", "k")
                if kind in (MID, PRE) and not (isinstance(b, int) and b == B - 1):
                    used, normed, nb = ahead(sp, it + CT, b * CT + CT, b + 1)
                    sp.wait_ge(xst_done, used)
                    sp.wait_ge(xlo_done, normed)
                    sp.dma_start(xs[:, 0, :], x_v[bass.ds(nb, 1), bass.ds(p, 1)]).then_inc(xst_load, 16)
                if nxt:
                    load_w(w_job(it, "k"), slot, "k")
                if kind == LAST:
                    load_norm_tile(b + 1, 4)
                    load_norm_tile(b + 1, 5)
                if kind == PRE:
                    used, nb = ahead(sp, it + (CT + 1), b + 1)
                    sp.wait_ge(xst_done, used)
                    sp.dma_start(xs[:, 0, :], x_v[bass.ds(nb, 1), CT - 1]).then_inc(xst_load, 16)
                sums_to_columns(it, 1, y_taken(it, Y[("sum", -1)]))
                if nxt:
                    load_w(w_job(it, "v"), slot, "v")
                    rotate(e, "q")
                spread_reciprocals(it, 1)
                if nxt:
                    load_w(w_job(it, "q"), p + 2, "q")
                    rotate(e, "k")
                store_output(it, 1)
                if nxt:
                    old, split = ahead(sp, it * STEPS + (STEPS // 2 + 1), e * 2 + 1)
                    sp.wait_ge(st_done, old)
                    spread(split, 0, "q")
                    spread(*ahead(sp, e * 2 + 2), 0, "k")
                if kind == PRE:
                    load_norm_tile(b + 1, 1, it + (CT + 2))
                    load_norm_tile(b + 1, 0)
                sums_to_columns(it, 0, y_taken(it, Y[("sum", 1)]))
                spread_reciprocals(it, 0)
                if kind == PRE:
                    load_norm_tile(b + 1, 2)
                    load_norm_tile(b + 1, 3)
                store_output(it, 0)

            each_iteration(sp, body)
            it = B * PAIRS
            sums_to_columns(it, 1, y_taken(it - 1, Y_LAST))
            spread_reciprocals(it, 1)
            store_output(it, 1)
            sp.wait_ge(od_store, it * 32 + 16)

        @block.gpsimd
        def _(pool):
            g = nc.gpsimd
            g.memset(ident[:], 0.0).then_inc(pool_setup, 1)
            g.memset(group[:], 1.0 / GROUP_P).then_inc(pool_setup, 1)
            g.memset(minus_half[:], -0.5).then_inc(pool_setup, 1)
            g.memset(acc_sum[:], 1.0).then_inc(fold_done, 1)
            g.memset(rows[:], 1.0).then_inc(acc_done, 3)
            g.memset(numer[:], 1.0).then_inc(out_done, 1)
            pool.wait_ge(pool_setup, 3)
            g.affine_select(out=ident[:], in_=ident[:], compare_op=ALU.not_equal, fill=1.0, base=0,
                            pattern=[[-1, P]], channel_multiplier=1).then_inc(pool_setup, 1)
            gv = group[:].rearrange("p (g j) -> p g j", j=GROUP_P)
            g.affine_select(out=gv, in_=gv, compare_op=ALU.is_ge, fill=0.0, base=0,
                            pattern=[[-GROUP_P, P // GROUP_P], [0, GROUP_P]],
                            channel_multiplier=1).then_inc(pool_setup, 1)
            pool.wait_ge(pool_setup, 5)
            g.affine_select(out=gv, in_=gv, compare_op=ALU.is_ge, fill=0.0, base=GROUP_P - 1,
                            pattern=[[GROUP_P, P // GROUP_P], [0, GROUP_P]],
                            channel_multiplier=-1).then_inc(pool_setup, 1)

            def split_w(job, o, free):
                pool.wait_ge(whi_done, job + 1)
                if free is not None:
                    pool.wait_ge(x_done, free)
                g.tensor_tensor(w_lo[:, W_BUF[o], :], w_raw[:], w_hi[:, W_BUF[o], :],
                                ALU.subtract).then_inc(wlo_done, 1)

            def rope(e, o):
                pool.wait_ge(rot_load[o], e * 64 + 64)
                g.tensor_tensor(raw[o][:], raw[o][:], cos2[:], ALU.mult).then_inc(mul1_done, 1)
                g.tensor_tensor(rot[:], rot[:], sin2[:], ALU.mult).then_inc(mul_done, 1)

            def add_up(it, s, Y):
                u, r = divmod(s, 4)
                if r == 0:
                    return
                pool.wait_ge(hi_done, it * STEPS + s + 1)
                if r == 1:
                    pool.wait_ge(fold_done, it * 4 + u + 1)
                    g.tensor_tensor(acc[:], p_hi[:, 0], p_hi[:, 1], ALU.add).then_inc(acc_done, 1)
                else:
                    pool.wait_ge(acc_done, it * 12 + 3 * u + r + 2)
                    g.tensor_tensor(acc[:], acc[:], p_hi[:, r], ALU.add).then_inc(acc_done, 1)
                if r == 3:
                    pool.wait_ge(acc_done, it * 12 + 3 * u + 6)
                    pool.wait_ge(y_done, y_count(it, Y[("sum", u - 1)]))
                    g.tensor_tensor(acc_sum[:], acc[:, 0], acc[:, 1], ALU.add).then_inc(fold_done, 1)

            def normalise(it, h, folds=None):
                if h == 1:
                    pool.wait_ge(fold_done, folds)
                pool.wait_ge(rb_load, it * 32 + (32 if h == 0 else 16))
                pool.wait_ge(u_free, it * 4 + (3 if h == 0 else 1))
                part = slice(h * D, h * D + D)
                g.tensor_tensor(recip_b[part, :], numer[part, :], recip_b[part, :],
                                ALU.mult).then_inc(out_done, 1)
                if h == 1:
                    pool.wait_ge(out_done, it * 2 + 2)

            def group_rstd(b):
                pool.wait_ge(gn_dve, b * 5 + 5)
                g.tensor_tensor(rstd[:], gvar[:], minus_half[:], ALU.pow).then_inc(gn_pool, 1)

            split_w(0, "q", None)
            group_rstd(0)
            split_w(1, "k", None)
            split_w(2, "v", 2)
            rope(0, "q")
            rope(0, "k")
            split_w(3, "q", 6)

            def body(it, b, p, kind):
                Y = y_index(kind)
                nxt = kind != FINAL
                for s in range(STEPS):
                    if nxt and s == 8:
                        rope(it + 1, "k")
                    if s + 1 < STEPS:
                        add_up(it, s + 1, Y)
                    if nxt and s == 2:
                        split_w(w_job(it, "k"), "k", it * 8 + 4)
                    if kind == PRE and s == 12:
                        group_rstd(b + 1)
                    if s == 6:
                        normalise(it, 1, it * 4 + 3)
                    if nxt and s == (6 if kind == LAST else 5):
                        rope(it + 1, "q")
                    if nxt and s == (5 if kind == LAST else 4):
                        split_w(w_job(it, "v"), "v", x_count(it, ("q", 1)))
                    if s == 14:
                        normalise(it, 0)
                    if nxt and s == 14:
                        split_w(w_job(it, "q"), "q", x_count(it, ("v", 1)))

            each_iteration(pool, body)
            normalise(B * PAIRS, 1, B * PAIRS * 4 + 1)

        @block.scalar
        def _(act):
            a = nc.scalar

            def split_w(job, o, free):
                act.wait_ge(w_load, job * 16 + 16)
                if free is not None:
                    act.wait_ge(x_done, free)
                a.copy(w_hi[:, W_BUF[o], :], w_raw[:]).then_inc(whi_done, 1)

            def exps(it, s):
                u, r = divmod(s, 4)
                act.wait_ge(st_done, it * STEPS + s + 2)
                act.wait_ge(pv_done, it * STEPS + s + 1)
                act.wait_ge(acc_done, it * 12 + 3 * u + max(r, 1))
                a.activation(p_hi[:, r], st[:, s % 2], ACT.Exp, scale=SCALE).then_inc(hi_done, 1)
                a.activation(st[:, s % 2], st[:, s % 2], ACT.Exp, scale=SCALE).then_inc(exp_done, 1)

            def evacuate(e, count, o, half):
                act.wait_ge(bias_done, e + 1)
                if o != "v" and half == 0 and not (isinstance(e, int) and e == 0):
                    act.wait_ge(qklo_done, e * 2 + ("qk".index(o) - 1))
                act.wait_ge(x_done, count)
                n = "qkv".index(o)
                a.activation(raw[o][:, half * Q:half * Q + Q], bx[:], ACT.Identity,
                             bias=bias_now[:, n:n + 1]).then_inc(x_free, 1)

            def round_qk(e, o):
                n = "qk".index(o)
                act.wait_ge(add_done, e * 2 + n + 1)
                if not (isinstance(e, int) and e == 0):
                    act.wait_ge(set_load[1], e * 96)
                a.copy(hi[o][:], raw[o][:]).then_inc(qkhi_done, 1)

            def v_hi(e, h, count, free):
                act.wait_ge(x_done, count)
                if free is not None:
                    act.wait_ge(pv_done, free)
                a.copy(vs[h][:, :, D:2 * D], bx[:].rearrange("p (t d) -> p t d", d=D)).then_inc(vhi_done, 1)

            def minus_max_row(e, h, half, count):
                act.wait_ge(y_done, count)
                a.copy(qb[h][D:D + 1, half * Q:half * Q + Q], by[D:D + 1, :]).then_inc(y_free, 1)

            def hi_sum_row(it, u, count):
                act.wait_ge(y_done, count)
                if u == 0:
                    act.wait_ge(cols_load, it * 64 + 32)
                elif u == 2:
                    act.wait_ge(cols_load, it * 64 + 64)
                half = u % 2
                a.copy(rows[0:1, half * Q:half * Q + Q], by[0:1, :]).then_inc(y_free, 1)

            def unit_out(it, u):
                act.wait_ge(pv_done, it * STEPS + 4 * u + 8)
                act.wait_ge(u_free, it * 4 + u + 1)
                a.copy(t1[:], u1[D:P, :]).then_inc(t1_done, 1)
                if u == 0:
                    act.wait_ge(cols_load, it * 64 + 32)
                elif u == 2:
                    act.wait_ge(cols_load, it * 64 + 64)
                half = u % 2
                a.copy(rows[D:D + 1, half * Q:half * Q + Q], u2[D:D + 1, :]).then_inc(lorow_done, 1)

            def round_x(b, t):
                act.wait_ge(xnorm_done, b * CT + t + 1)
                a.copy(xn_hi[:, t, :], x_tile(b, t)).then_inc(xhi_done, 1)

            def round_tiles(b, s, kind):
                for t in SPLIT[kind].get(s, ()):
                    round_x(b + 1, t)

            split_w(0, "q", None)
            for t in range(CT):
                round_x(0, t)
            split_w(1, "k", None)
            act.wait_ge(consts_dma, 80)
            act.wait_ge(dve_setup, DVE_SETUP)
            act.wait_ge(pool_setup, POOL_SETUP)
            evacuate(0, 1, "q", 0)
            evacuate(0, 2, "q", 1)
            split_w(2, "v", 2)
            evacuate(0, 3, "k", 0)
            evacuate(0, 4, "k", 1)
            round_qk(0, "q")
            evacuate(0, 5, "v", 0)
            evacuate(0, 6, "v", 1)
            round_qk(0, "k")
            v_hi(0, 0, 7, None)
            split_w(3, "q", 6)
            minus_max_row(0, 0, 0, Y_FIRST - 2)
            exps(0, 0)

            def body(it, b, p, kind):
                Y, plan = y_index(kind), y_plan(kind)
                nxt = kind != FINAL
                e = it + 1
                for s in range(STEPS):
                    if s == 0:
                        v_hi(it, 1, x_count(it, ("tr", 1)), it * STEPS + 4)
                    if s < STEPS - 1 or nxt:
                        exps(it, s + 1)
                    ended = EVAC[kind].get(s)
                    early = ended and ended not in [job[:2] for job in X_PLAN[kind][s][1]]
                    if early:
                        evacuate(e, x_count(it, ended), *ended)
                    if nxt and s == (8 if kind == LAST else 7):
                        round_qk(e, "q")
                    if nxt and s == 9:
                        round_qk(e, "k")
                    if kind == LAST:
                        round_tiles(b, s, kind)
                    for j in [j for place in plan[s] for j in place]:
                        if j[0] == "row":
                            minus_max_row(e if j[-1] else it, j[1], j[2], y_count(it, Y[j]))
                        elif j[0] == "sum":
                            hi_sum_row(it, j[1], y_count(it, Y[j]))
                    if kind == PRE:
                        round_tiles(b, s, kind)
                    if s % 4 == 3:
                        unit_out(it, s // 4)
                    if ended and not early:
                        evacuate(e, x_count(it, ended), *ended)
                    if nxt and s == 2:
                        split_w(w_job(it, "k"), "k", it * 8 + 4)
                    if nxt and s == (5 if kind == LAST else 4):
                        split_w(w_job(it, "v"), "v", x_count(it, ("q", 1)))
                    if nxt and s == 13:
                        split_w(w_job(it, "q"), "q", x_count(it, ("v", 1)))
                    if nxt and s == 14:
                        v_hi(e, 0, x_count(it, ("tr", 0)), it * STEPS + 12)

            each_iteration(act, body)
            hi_sum_row(B * PAIRS, -1, y_count(B * PAIRS - 1, Y_LAST))

        @block.vector
        def _(dve):
            v = nc.vector

            def bn_halves(tile, k):
                v.bn_stats(stats[:, bass.ds(k * 2, 1), :], tile[:, 0:Q])
                v.bn_stats(stats[:, bass.ds(k * 2 + 1, 1), :], tile[:, Q:N]).then_inc(xst_done, 1)

            def tile_stats(n, k):
                dve.wait_ge(xst_load, n * 16 + 16)
                bn_halves(xs[:, 0, :], k)

            def partition_stats(b, n):
                dve.wait_ge(xst_done, n)
                v.memset(gdev[:], 0.0)
                v.bn_aggr(mv[:], stats[:].rearrange("p k s -> p (k s)")).then_inc(gn_dve, 1)

            def group_mean(b):
                dve.wait_ge(gn_pe, b * 2 + 1)
                v.tensor_copy(gmean[:], by[:, 0:1]).then_inc(gn_dve, 1)
                dve.wait_ge(gn_dve, b * 5 + 2)
                v.tensor_tensor(gdev[:, 0:1], mv[:, 0:1], gmean[:], ALU.subtract).then_inc(gn_dve, 1)
                dve.wait_ge(gn_dve, b * 5 + 3)
                v.scalar_tensor_tensor(gdev[:, 1:2], gdev[:, 0:1], gdev[:, 0:1], mv[:, 1:2],
                                       ALU.mult, ALU.add).then_inc(gn_dve, 1)

            def group_variance(b):
                dve.wait_ge(gn_pe, b * 2 + 2)
                v.tensor_scalar(gvar[:], by[:, 2:3], EPS, None, ALU.add).then_inc(gn_dve, 1)

            def norm_tile(b, t):
                if t == 0:
                    dve.wait_ge(gn_pool, b + 1)
                if not (isinstance(b, int) and b == 0):
                    dve.wait_ge(xn_load[t % 2], b * 48 + (16 * (t // 2) - 32))
                v.tensor_scalar(x_tile(b, t), x_tile(b, t), gmean[:], rstd[:],
                                ALU.subtract, ALU.mult).then_inc(xnorm_done, 1)

            def x_lo(b, t):
                dve.wait_ge(xhi_done, b * CT + t + 1)
                v.tensor_tensor(xn_lo[:, t, :], x_tile(b, t), xn_hi[:, t, :],
                                ALU.subtract).then_inc(xlo_done, 1)

            def pair_bias(pair):
                v.tensor_copy(bias_now[:], bias[:, bass.ds(pair, 1), :]).then_inc(bias_done, 1)

            def p_low(it, s):
                dve.wait_ge(exp_done, it * STEPS + s + 1)
                dve.wait_ge(pv_done, it * STEPS + s + 3)
                v.tensor_tensor(p_lo[:, s % 2], st[:, s % 2], p_hi[:, s % 4],
                                ALU.subtract).then_inc(lo_done, 1)

            def rope_add(e, o):
                n = "qk".index(o)
                dve.wait_ge(mul1_done, e * 2 + n + 1)
                dve.wait_ge(mul_done, e * 2 + n + 1)
                v.tensor_tensor(raw[o][:], raw[o][:], rot[:], ALU.add).then_inc(add_done, 1)

            def qk_lo(e, o):
                n = "qk".index(o)
                dve.wait_ge(qkhi_done, e * 2 + n + 1)
                v.tensor_tensor(lo[o][:], raw[o][:], hi[o][:], ALU.subtract).then_inc(qklo_done, 1)

            def v_lo(e, h):
                dve.wait_ge(vhi_done, e * 2 + h + 1)
                v.tensor_tensor(vs[h][:, :, 0:D], bx[:].rearrange("p (t d) -> p t d", d=D),
                                vs[h][:, :, D:2 * D], ALU.subtract).then_inc(x_free, 1)

            def maximum(count, i):
                dve.wait_ge(y_done, count)
                v.tensor_reduce(maxes[:, i // 2, i % 2:i % 2 + 1], by[:], AX.X, ALU.max,
                                negate=True).then_inc(y_free, 1)
                if i == 7:
                    dve.wait_ge(y_free, count + 1)
                    v.tensor_tensor(neg_m[:], maxes[:, :, 0], maxes[:, :, 1], ALU.min).then_inc(negm_done, 1)

            def unit_sum(it, u):
                h, half = divmod(u, 2)
                dve.wait_ge(t1_done, it * 4 + u + 1)
                v.tensor_tensor(t1[:], u1[0:D, :], t1[:], ALU.add).then_inc(t2_done, 1)
                dve.wait_ge(t2_done, it * 4 + u + 1)
                if u == 0:
                    dve.wait_ge(out_done, it * 2 + 1)
                elif u == 2:
                    dve.wait_ge(out_done, it * 2 + 2)
                v.tensor_tensor(numer[h * D:h * D + D, half * Q:half * Q + Q], u2[0:D, :], t1[:],
                                ALU.add).then_inc(u_free, 1)

            def reciprocals(it, h):
                n = it * 2 + (2 if h == 0 else 1)
                dve.wait_ge(cols_load, it * 64 + (64 if h == 0 else 32))
                v.tensor_tensor(cols[:, 0, :], cols[:, 0, :], cols[:, 1, :], ALU.add).then_inc(colsum_done, 1)
                dve.wait_ge(colsum_done, n)
                v.reciprocal(cols_inv[:], cols[:, 0, :]).then_inc(recip_done, 1)

            v.memset(ones[:], 1.0).then_inc(dve_setup, 1)
            for h in range(2):
                v.memset(vs[h][:, :, 2 * D:3 * D].bitcast(fp32), 1.0).then_inc(dve_setup, 1)
                v.memset(kb[h][D:D + 1, :].bitcast(fp32), 1.0).then_inc(dve_setup, 1)
            v.memset(cols_inv[0:1, 0:1], 1.0).then_inc(st_done, 1)
            v.memset(cols_inv[0:1, 1:2], 1.0).then_inc(lo_done, 2)
            v.memset(cols_inv[0:1, 2:3], 1.0).then_inc(pv_done, 4)
            v.memset(cols_inv[0:1, 3:4], 1.0).then_inc(y_free, 1)
            v.memset(cols_inv[0:1, 4:5], 1.0).then_inc(x_free, 1)
            v.memset(cols_inv[0:1, 5:6], 1.0).then_inc(u_free, 1)
            v.memset(cols_inv[0:1, 6:7], 1.0).then_inc(lorow_done, 1)
            dve.wait_ge(pool_setup, POOL_SETUP)
            v.tensor_copy(ident_r[:], ident[:]).then_inc(dve_setup, 1)
            for t in range(CT // 2):
                dve.wait_ge(x0_load[t], 16)
                bn_halves(x_tile(0, t), t)
            dve.wait_ge(consts_dma, 80)
            for h in range(2):
                v.tensor_scalar(sin2[h * D:h * D + 32, :], sin2[h * D:h * D + 32, :], -1.0, None,
                                ALU.mult).then_inc(dve_setup, 1)
            pair_bias(0)
            for t in range(CT // 2, CT):
                dve.wait_ge(x0_load[t], 16)
                bn_halves(x_tile(0, t), t)
            partition_stats(0, CT)
            group_mean(0)
            group_variance(0)
            for t in range(CT):
                norm_tile(0, t)
                if t >= 1:
                    x_lo(0, t - 1)
            x_lo(0, CT - 1)
            rope_add(0, "q")
            qk_lo(0, "q")
            rope_add(0, "k")
            qk_lo(0, "k")
            v_lo(0, 0)
            for i in range(8):
                maximum(i + 1, i)
            p_low(0, 0)
            for i in range(2):
                maximum(Y_FIRST - 1 + i, i)

            def body(it, b, p, kind):
                Y, plan = y_index(kind), y_plan(kind)
                nxt = kind != FINAL
                e = it + 1

                def maxima(jobs):
                    for j in jobs:
                        if j[0] == "max":
                            maximum(y_count(it, Y[j]), j[3])

                for s in range(STEPS):
                    if kind == PRE and s == 11:
                        group_mean(b + 1)
                    if kind == PRE and s == 12:
                        group_variance(b + 1)
                    maxima(plan[s][0])
                    if s == 0:
                        v_lo(it, 1)
                    if nxt and s == 9:
                        rope_add(e, "k")
                    maxima(plan[s][1])
                    if s < STEPS - 1 or nxt:
                        p_low(it, s + 1)
                    maxima(plan[s][2] + plan[s][3])
                    if nxt and s == 8:
                        qk_lo(e, "q")
                    if nxt and s == 9:
                        qk_lo(e, "k")
                    if nxt and s == 0:
                        pair_bias(0 if kind == LAST else p + 1)
                    for t in NORM[kind].get(s, ()):
                        norm_tile(b + 1, t)
                    for t in SPLIT[kind].get(s, ()):
                        x_lo(b + 1, t)
                    if s == 4:
                        reciprocals(it, 1)
                    if kind == MID and s == 10 and not (isinstance(b, int) and b == B - 1):
                        tile_stats(it, p)
                    if kind == PRE and s == 2:
                        tile_stats(it, CT - 2)
                    if kind == PRE and s == 10:
                        tile_stats(it + 1, CT - 1)
                        partition_stats(b + 1, it + (CT + 2))
                    if s == 13:
                        reciprocals(it, 0)
                    if s % 4 == 3:
                        unit_sum(it, s // 4)
                    if nxt and s == (7 if kind == LAST else 6):
                        rope_add(e, "q")
                    if nxt and s == 14:
                        v_lo(e, 0)

            each_iteration(dve, body)
            reciprocals(B * PAIRS, 1)

        @block.tensor
        def _(pe):
            t_ = nc.tensor

            def project(e, o, half, first, last, xc, w):
                for i in range(first, last):
                    t, kind = divmod(i, 3)
                    if i == 0:
                        pe.wait_ge(x_free, xc)
                        pe.wait_ge(wlo_done, w + 1)
                    wt, xt = ((w_hi, xn_hi), (w_hi, xn_lo), (w_lo, xn_hi))[kind]
                    m = t_.matmul(bx[:], wt[:, W_BUF[o], t * P:t * P + P], xt[:, t, half * Q:half * Q + Q],
                                  start=i == 0, stop=i == PROD - 1)
                    if i == PROD - 1:
                        m.then_inc(x_done, 1)

            def transpose_v(h, xc):
                pe.wait_ge(x_free, xc)
                part = slice(h * D, h * D + D)
                t_.matmul(bx[:, 0:D], raw["v"][part, 0:P], ident[part, part], start=True, stop=True)
                for t in range(1, KT):
                    m = t_.transpose(bx[:, t * D:t * D + D], raw["v"][part, t * P:t * P + P], ident[part, part])
                m.then_inc(x_done, 1)

            def group_average(b, part, yc=None):
                if yc is not None:
                    pe.wait_ge(y_free, yc)
                pe.wait_ge(gn_dve, b * 5 + (4 if part else 1))
                src, col = (gdev[:, 1:2], 2) if part else (mv[:, 0:1], 0)
                t_.matmul(by[:, col:col + 1], group[:], src, start=True, stop=True).then_inc(gn_pe, 1)

            def scores(it, s):
                h, half, kp = s // 8 % 2, s // 4 % 2, s % 4
                if s % 4 == 0:
                    pe.wait_ge(set_load[h], (it + s // STEPS) * 96 + 96)
                    if s % STEPS == 0:
                        pe.wait_ge(y_free, y_taken(it + s // STEPS - 1, ROW_0))
                    else:
                        pe.wait_ge(y_free, y_taken(it, y_index(MID)[("row", h, half, False)]))
                pe.wait_ge(lo_done, it * STEPS + s + 1)
                for j in range(2):
                    key = slice((2 * kp + j) * P, (2 * kp + j) * P + P)
                    qs = slice(half * Q, half * Q + Q)
                    t_.matmul(st[:, s % 2, j, :], ka[h][:, key], qa[h][:, qs], start=True, stop=False)
                    m = t_.matmul(st[:, s % 2, j, :], kb[h][0:D + 1, key], qb[h][0:D + 1, qs],
                                  start=False, stop=True)
                m.then_inc(st_done, 1)

            def values(it, s):
                u, kp = divmod(s, 4)
                h = u // 2
                if kp == 0:
                    if u == 0:
                        pe.wait_ge(x_free, x_taken(it - 1, ("tr", 0)))
                    elif u == 2:
                        pe.wait_ge(x_free, x_taken(it, ("tr", 1)))
                    pe.wait_ge(u_free, it * 4 + u + 1)
                    pe.wait_ge(lorow_done, it * 4 + u + 1)
                pe.wait_ge(hi_done, it * STEPS + s + 1)
                for j in range(2):
                    t_.matmul(u1[:], vs[h][:, 2 * kp + j, 0:2 * D], p_hi[:, s % 4, j, :],
                              start=kp == 0 and j == 0, stop=kp == 3 and j == 1)
                pe.wait_ge(lo_done, it * STEPS + s + 3)
                for j in range(2):
                    m = t_.matmul(u2[:], vs[h][:, 2 * kp + j, D:3 * D], p_lo[:, s % 2, j, :],
                                  start=kp == 0 and j == 0, stop=kp == 3 and j == 1)
                m.then_inc(pv_done, 1)

            def y_job(it, e, j, count):
                pe.wait_ge(y_free, count)
                if j[0] == "max":
                    _, h, half, i, _ = j
                    if i == 0 and half == 0:
                        pe.wait_ge(set_load[h], e * 96 + 96)
                    qt, kh = half * 4 + i // 2, i % 2
                    m = t_.matmul(by[:], qa[h][:, qt * P:qt * P + P], ka[h][:, kh * Q:kh * Q + Q],
                                  start=True, stop=True)
                elif j[0] == "row":
                    _, h, half, _ = j
                    pe.wait_ge(negm_done, e * 4 + 2 * h + half + 1)
                    for i in range(4):
                        m = t_.matmul(by[:, i * P:i * P + P], neg_m[:, i:i + 1].to_broadcast([P, P]),
                                      ident_r[:], start=True, stop=True)
                else:
                    pe.wait_ge(fold_done, it * 4 + j[1] + 2)
                    m = t_.matmul(by[:], ones[:], acc_sum[:], start=True, stop=True)
                m.then_inc(y_done, 1)

            pe.wait_ge(pool_setup, POOL_SETUP)
            group_average(0, 0)
            group_average(0, 1)
            pe.wait_ge(dve_setup, DVE_SETUP)
            for t in range(CT):
                pe.wait_ge(xlo_done, t + 1)
                project(0, "q", 0, 3 * t, 3 * t + 3, 1, 0)
            for n, (o, half) in enumerate([("q", 1), ("k", 0), ("k", 1), ("v", 0), ("v", 1)], 1):
                project(0, o, half, 0, PROD, n + 1, n // 2)
            transpose_v(0, X_FIRST)
            for i in range(8):
                y_job(0, 0, ("max", 0, 0, i, False), i + 1)
            y_job(0, 0, ("row", 0, 0, False), Y_FIRST - 2)
            scores(0, 0)
            for i in range(2):
                y_job(0, 0, ("max", 0, 1, i, False), Y_FIRST - 1 + i)

            def body(it, b, p, kind):
                Y, plan = y_index(kind), y_plan(kind)
                e = it + 1
                done = {}

                def projections(s, part):
                    for o, half, n in X_PLAN[kind].get(s, ([], []))[part]:
                        i = done.get((o, half), 0)
                        w = it * 3 + {"q": 3, "k": 4, "v": 5}[o]
                        done[(o, half)] = i + n
                        while i < done[(o, half)]:
                            m = n
                            if kind == LAST and (o, half) == ("q", 0):
                                pe.wait_ge(xlo_done, b * CT + (CT + i // 3 + 1))
                                m = 3
                            project(e, o, half, i, i + m, x_count(it, (o, half)), w)
                            i += m

                def y_jobs(jobs):
                    for j in jobs:
                        y_job(it, e if j[-1] is True else it, j, y_count(it, Y[j]))

                for s in range(STEPS):
                    if s == 0:
                        transpose_v(1, x_count(it, ("tr", 1)))
                    if s < STEPS - 1 or kind != FINAL:
                        scores(it, s + 1)
                    if kind == PRE and s == 12:
                        pe.wait_ge(gn_dve, (b + 1) * 5 + 5)
                    y_jobs(plan[s][0])
                    projections(s, 0)
                    if kind != FINAL and s == 14:
                        transpose_v(0, x_count(it, ("tr", 0)))
                    y_jobs(plan[s][1])
                    values(it, s)
                    if kind == PRE and s == 11:
                        pe.wait_ge(gn_dve, (b + 1) * 5 + 2)
                    y_jobs(plan[s][2])
                    projections(s, 1)
                    y_jobs(plan[s][3])
                    if kind == PRE and s == 10:
                        group_average(b + 1, 0, y_taken(it, Y[("sum", 1)]))
                    if kind == PRE and s == 11:
                        group_average(b + 1, 1, y_taken(it, Y[("max", 0, 0, 0, True)]))

            each_iteration(pe, body)
            last = B * PAIRS - 1
            y_job(last, last, ("sum", 3), y_count(last, Y_LAST))


def phase2(nc, xT, wp, bp, od, out):
    fp32, f32r = mybir.dt.float32, mybir.dt.float32r
    ALU = mybir.AluOpType
    wp_v = wp.rearrange("(t p) n -> p t n", p=P)
    x_v = xT.rearrange("b (t p) n -> b p t n", p=P)
    out_v = out.rearrange("b (t p) n -> b p t n", p=P)
    od_v = od.rearrange("s p n -> p s n")

    with ExitStack() as ctx:
        def sb(name, shape, dt=fp32):
            return ctx.enter_context(nc.sbuf_tensor(name, shape, dt))

        def sem(name):
            return ctx.enter_context(nc.semaphore(name))

        w_raw = sb("wp_raw", [P, CT, C])
        w_hi, w_lo = sb("wp_hi", [P, CT, C], f32r), sb("wp_lo", [P, CT, C], f32r)
        bias = sb("bias_p", [P, CT])
        att = [sb(f"att{h}", [P, CT, Q]) for h in range(2)]
        att_hi = [sb(f"att_hi{h}", [P, CT, Q], f32r) for h in range(2)]
        att_lo = [sb(f"att_lo{h}", [P, CT, Q], f32r) for h in range(2)]
        res = [sb(f"res{h}", [P, CT, Q]) for h in range(2)]
        banks = [ctx.enter_context(nc.psum_tensor(f"proj{c}", [P, Q], fp32)) for c in range(CT)]

        w_load = [sem(f"wp_load{t}") for t in range(CT)]
        att_first = [sem(f"att_first{t}") for t in range(CT)]
        bias_load = sem("bias_load")
        w_hi_done, w_lo_done = sem("wp_hi_done"), sem("wp_lo_done")
        first_hi, first_lo = sem("first_hi"), sem("first_lo")
        att_load = [sem(f"att_load{h}") for h in range(2)]
        res_load = [sem(f"res_load{h}") for h in range(2)]
        out_store = [sem(f"out_store{h}") for h in range(2)]
        hi_done, lo_done = sem("att_hi_done"), sem("att_lo_done")
        proj_done, out_done = sem("proj_done"), sem("proj_out")

        block = ctx.enter_context(nc.Block())

        @block.sync
        def _(sp):
            for t in range(CT):
                sp.dma_start(w_raw[:, t, :], wp_v[:, t, :]).then_inc(w_load[t], 16)
                sp.dma_start(att[0][:, t, :], od_v[:, 1 + t, 0:Q]).then_inc(att_first[t], 16)
            sp.dma_start(bias[:], bp).then_inc(bias_load, 16)

            def load(b, h, first):
                cols = slice(h * Q, h * Q + Q)
                b, slot, split, stored = ahead(sp, b, b * PAIRS + 1, b * 2 + (h - 2), b * 16)
                if not first:
                    sp.wait_ge(lo_done, split)
                if not (first and h == 0):
                    sp.dma_start(att[h][:], od_v[:, bass.ds(slot, PAIRS), cols]).then_inc(att_load[h], 16)
                if not first:
                    sp.wait_ge(out_store[h], stored)
                sp.dma_start(res[h][:], x_v[bass.ds(b, 1), :, :, cols]).then_inc(res_load[h], 16)

            def store(b, h):
                b, done = ahead(sp, b, b * 12 + (6 * h + 6))
                sp.wait_ge(out_done, done)
                sp.dma_start(out_v[bass.ds(b, 1), :, :, h * Q:h * Q + Q], res[h][:]).then_inc(out_store[h], 16)

            load(0, 0, True)
            load(0, 1, True)
            with sp.Fori(0, B - 1) as b:
                for h in range(2):
                    store(b, h)
                    load(b + 1, h, False)
            for h in range(2):
                store(B - 1, h)
            for h in range(2):
                sp.wait_ge(out_store[h], B * 16)

        @block.scalar
        def _(act):
            for t in range(CT):
                act.wait_ge(w_load[t], 16)
                nc.scalar.copy(w_hi[:, t, :], w_raw[:, t, :]).then_inc(w_hi_done, 1)
                act.wait_ge(att_first[t], 16)
                nc.scalar.copy(att_hi[0][:, t, :], att[0][:, t, :]).then_inc(first_hi, 1)

            def split(b, h, first):
                act.wait_ge(att_load[h], b * 16 if h == 0 else b * 16 + 16)
                if not first:
                    act.wait_ge(proj_done, b * 12 + (6 * h - 6))
                nc.scalar.copy(att_hi[h][:], att[h][:]).then_inc(hi_done, 1)

            split(0, 1, True)
            with act.Fori(1, B) as b:
                for h in range(2):
                    split(b, h, False)

        @block.vector
        def _(dve):
            for t in range(CT):
                dve.wait_ge(w_hi_done, t + 1)
                nc.vector.tensor_tensor(w_lo[:, t, :], w_raw[:, t, :], w_hi[:, t, :],
                                        ALU.subtract).then_inc(w_lo_done, 1)
                dve.wait_ge(first_hi, t + 1)
                nc.vector.tensor_tensor(att_lo[0][:, t, :], att[0][:, t, :], att_hi[0][:, t, :],
                                        ALU.subtract).then_inc(first_lo, 1)
            dve.wait_ge(bias_load, 16)

            def split(b, h, first):
                dve.wait_ge(hi_done, b * 2 + h)
                if not first:
                    dve.wait_ge(proj_done, b * 12 + (6 * h - 6))
                nc.vector.tensor_tensor(att_lo[h][:], att[h][:], att_hi[h][:], ALU.subtract).then_inc(lo_done, 1)

            def finish(b, h):
                dve.wait_ge(res_load[h], b * 16 + 16)
                for c in range(CT):
                    dve.wait_ge(proj_done, b * 12 + (6 * h + c + 1))
                    nc.vector.scalar_tensor_tensor(res[h][:, c, :], banks[c][:], bias[:, c:c + 1], res[h][:, c, :],
                                                   ALU.add, ALU.add).then_inc(out_done, 1)

            split(0, 1, True)
            with dve.Fori(0, B - 1) as b:
                for h in range(2):
                    finish(b, h)
                    split(b + 1, h, False)
            for h in range(2):
                finish(B - 1, h)

        @block.tensor
        def _(pe):
            def products(h, c, t):
                for w, a in ((w_hi, att_hi), (w_hi, att_lo), (w_lo, att_hi)):
                    m = nc.tensor.matmul(banks[c][:], w[:, t, c * P:c * P + P], a[h][:, t, :],
                                         start=t == 0 and w is w_hi and a is att_hi,
                                         stop=t == CT - 1 and w is w_lo)
                return m

            def first_unit():
                for t in range(CT):
                    pe.wait_ge(w_lo_done, t + 1)
                    pe.wait_ge(first_lo, t + 1)
                    for c in range(CT):
                        m = products(0, c, t)
                        if t == CT - 1:
                            m.then_inc(proj_done, 1)

            def unit(b, h):
                pe.wait_ge(lo_done, b * 2 + h)
                for c in range(CT):
                    pe.wait_ge(out_done, b * 12 + (6 * h + c - 5))
                    for t in range(CT):
                        m = products(h, c, t)
                    m.then_inc(proj_done, 1)

            first_unit()
            unit(0, 1)
            with pe.Fori(1, B) as b:
                for h in range(2):
                    unit(b, h)


def build(nc, xT, wqkv, bqkv, ropeT, wp, bp, out):
    fp32 = mybir.dt.float32
    od = nc.dram_tensor("attention_out", [B * PAIRS + 1, P, N], fp32, kind="Internal").ap()
    rd = nc.dram_tensor("reciprocals", [N], fp32, kind="Internal").ap()
    phase1(nc, xT, wqkv, bqkv, ropeT, od, rd)
    phase2(nc, xT, wp, bp, od, out)


def kernel(x, L0_conv_rope, L0_conv_qkv_w, L0_conv_qkv_b, L0_conv_proj_w, L0_conv_proj_b):
    import numpy as np
    import concourse.bacc as bacc
    from concourse.bass_utils import run_bass_kernel_spmd

    xT = np.ascontiguousarray(np.asarray(x).reshape(B, N, C).transpose(0, 2, 1))
    w = np.asarray(L0_conv_qkv_w).reshape(C, 3, PAIRS, P).transpose(2, 1, 0, 3)
    arrays = {
        "xT": xT,
        "wqkv": np.ascontiguousarray(np.concatenate([w, w[:2]], axis=0)),
        "bqkv": np.ascontiguousarray(np.asarray(L0_conv_qkv_b).reshape(3, PAIRS, P).transpose(2, 1, 0).reshape(P, -1)),
        "ropeT": np.ascontiguousarray(np.asarray(L0_conv_rope).T),
        "wp": np.ascontiguousarray(np.asarray(L0_conv_proj_w)),
        "bp": np.ascontiguousarray(np.asarray(L0_conv_proj_b).reshape(CT, P).T),
    }
    nc = bacc.Bacc("TRN2", target_bir_lowering=False, num_devices=1)
    args = [nc.dram_tensor(n, v.shape, mybir.dt.from_np(v.dtype), kind="ExternalInput").ap()
            for n, v in arrays.items()]
    out = nc.dram_tensor("yT", [B, C, N], mybir.dt.float32, kind="ExternalOutput").ap()
    build(nc, *args, out)
    r = run_bass_kernel_spmd(nc, [arrays], core_ids=[0])
    y = r.results[0]["yT"]
    return np.ascontiguousarray(y.transpose(0, 2, 1)).reshape(x.shape)
```
